# Optimizing a Trainium2 kernel written in Bass

```python
import numpy as np
import jax
import jax.numpy as jnp

def _softmax(x, axis=-1):
    return jax.nn.softmax(x, axis=axis)

def _gelu(x):
    return jax.nn.gelu(x, approximate=True)

def _silu(x):
    return jax.nn.silu(x)

def _sigmoid(x):
    return jax.nn.sigmoid(x)

def _layernorm(x, axis=-1, eps=1e-05):
    m = jnp.mean(x, axis=axis, keepdims=True)
    v = jnp.var(x, axis=axis, keepdims=True)
    return (x - m) / jnp.sqrt(v + eps)

def _scatter_add(tgt, idx, src, axis=0):
    return tgt.at[idx].add(src)

def _segment_sum(src, seg, n):
    return jax.ops.segment_sum(src, seg, n)
kernel_name = 'mk_gnn_preln_d2_gnn_r8_f19c20'

def setup_inputs(seed: int=0):
    np.random.seed(seed)
    _w = jnp.asarray

    def _rec_inputs():
        import jax
        import jax.numpy as jnp
        _gk = jax.random.key(seed)
        x = -0.000202 + 1 * jax.random.normal(jax.random.fold_in(_gk, 1), (6250, 128), jnp.float32)
        _s = jax.random.randint(jax.random.fold_in(_gk, 2), (100000,), 0, 6250, jnp.int32)
        _d = jax.random.randint(jax.random.fold_in(_gk, 3), (100000,), 0, 6250, jnp.int32)
        _loop = jnp.arange(6250, dtype=jnp.int32)
        src = jnp.concatenate([_s, _d, _loop])
        dst = jnp.concatenate([_d, _s, _loop])
        _o = jnp.argsort(dst, stable=True)
        src = src[_o]
        dst = dst[_o]
        edge_attr_64 = 0.000189758 + 1.00013 * jax.random.normal(jax.random.fold_in(_gk, 12), (206250, 64), jnp.float32)
        return (x, src, dst, edge_attr_64)
    x, src, dst, edge_attr_64 = _rec_inputs()

    def _L0_gnn_setup():
        import jax, jax.numpy as jnp
        import numpy as np
        N, E, IN, HID = (6250, 200000, 128, 128)

        def _gcn(x, W, b, src, dst, norm):
            h = x @ W
            msg = h[src] * norm[:, None]
            out = jax.ops.segment_sum(msg, dst, num_segments=N)
            return out + b
        key = jax.random.key(seed)
        k0, k1, k2, k3 = jax.random.split(key, 4)
        x = jax.random.normal(k0, (N, IN), dtype=jnp.float32)
        edges = jax.random.randint(k1, (2, E), 0, N, dtype=jnp.int64)
        W1 = jax.random.normal(k2, (IN, HID), dtype=jnp.float32) * (1.0 / np.sqrt(IN))
        b1 = jnp.zeros((HID,), jnp.float32)
        W2 = jax.random.normal(k3, (HID, IN), dtype=jnp.float32) * (1.0 / np.sqrt(HID))
        b2 = jnp.zeros((IN,), jnp.float32)
        return {'x': x, 'edges': edges, 'W1': W1, 'b1': b1, 'W2': W2, 'b2': b2}
    _L0_gnn_all = _L0_gnn_setup()
    _L0_gnn_in = {k: v for k, v in _L0_gnn_all.items() if k in ('W1', 'b1', 'W2', 'b2')}
    del _L0_gnn_all

    def _L1_gnn_setup():
        import jax, jax.numpy as jnp
        import numpy as np
        N_NODES = 6250
        N_EDGES = 100000
        N_GRAPHS = 64
        NEG_SLOPE = 0.01

        def leaky_relu(x):
            return jnp.where(x >= 0, x, NEG_SLOPE * x)
        key = jax.random.key(seed)
        ks = jax.random.split(key, 10)
        x = jax.random.normal(ks[0], (N_NODES, 128), dtype=jnp.float32)
        edge_index = jax.random.randint(ks[1], (2, N_EDGES), 0, N_NODES, dtype=jnp.int64)
        edge_attr = jax.random.normal(ks[2], (N_EDGES, 64), dtype=jnp.float32)
        u = jax.random.normal(ks[3], (N_GRAPHS, 64), dtype=jnp.float32)
        batch = jnp.sort(jax.random.randint(ks[4], (N_NODES,), 0, N_GRAPHS, dtype=jnp.int64))
        s1 = 1.0 / np.sqrt(256)
        w1 = jax.random.uniform(ks[5], (256, 256), jnp.float32, -s1, s1)
        b1 = jnp.zeros((256,), jnp.float32)
        w2 = jax.random.uniform(ks[6], (256, 256), jnp.float32, -s1, s1)
        b2 = jnp.zeros((256,), jnp.float32)
        w3 = jax.random.uniform(ks[7], (256, 128), jnp.float32, -s1, s1)
        b3 = jnp.zeros((128,), jnp.float32)
        return {'x': x, 'edge_index': edge_index, 'edge_attr': edge_attr, 'u': u, 'batch': batch, 'w1': w1, 'b1': b1, 'w2': w2, 'b2': b2, 'w3': w3, 'b3': b3}
    _L1_gnn_all = _L1_gnn_setup()
    _L1_gnn_in = {k: v for k, v in _L1_gnn_all.items() if k in ('u', 'w1', 'b1', 'w2', 'b2', 'w3', 'b3')}
    del _L1_gnn_all
    return {'x': x, 'src': src, 'dst': dst, 'edge_attr_64': edge_attr_64, 'L0_gnn_W1': _L0_gnn_in['W1'], 'L0_gnn_b1': _L0_gnn_in['b1'], 'L0_gnn_W2': _L0_gnn_in['W2'], 'L0_gnn_b2': _L0_gnn_in['b2'], 'L1_gnn_u': _L1_gnn_in['u'], 'L1_gnn_w1': _L1_gnn_in['w1'], 'L1_gnn_b1': _L1_gnn_in['b1'], 'L1_gnn_w2': _L1_gnn_in['w2'], 'L1_gnn_b2': _L1_gnn_in['b2'], 'L1_gnn_w3': _L1_gnn_in['w3'], 'L1_gnn_b3': _L1_gnn_in['b3']}

def reference(x, src, dst, edge_attr_64, L0_gnn_W1, L0_gnn_b1, L0_gnn_W2, L0_gnn_b2, L1_gnn_u, L1_gnn_w1, L1_gnn_b1, L1_gnn_w2, L1_gnn_b2, L1_gnn_w3, L1_gnn_b3):
    import jax
    import jax.numpy as jnp

    def _L0_gnn_ref(x, edges, W1, b1, W2, b2):
        import jax, jax.numpy as jnp
        import numpy as np
        N, E, IN, HID = (6250, 200000, 128, 128)

        def _gcn(x, W, b, src, dst, norm):
            h = x @ W
            msg = h[src] * norm[:, None]
            out = jax.ops.segment_sum(msg, dst, num_segments=N)
            return out + b
        self_loop = jnp.arange(N, dtype=edges.dtype)
        src = jnp.concatenate([edges[0], self_loop])
        dst = jnp.concatenate([edges[1], self_loop])
        deg = jax.ops.segment_sum(jnp.ones_like(dst, dtype=x.dtype), dst, num_segments=N)
        dis = jax.lax.rsqrt(jnp.maximum(deg, 1.0))
        norm = dis[src] * dis[dst]
        h = jax.nn.relu(_gcn(x, W1, b1, src, dst, norm))
        h = jax.nn.relu(_gcn(h, W2, b2, src, dst, norm))
        return (x + h) * 0.5

    def _L1_gnn_ref(x, edge_index, edge_attr, u, batch, w1, b1, w2, b2, w3, b3):
        import jax, jax.numpy as jnp
        import numpy as np
        N_NODES = 6250
        N_EDGES = 100000
        N_GRAPHS = 64
        NEG_SLOPE = 0.01

        def leaky_relu(x):
            return jnp.where(x >= 0, x, NEG_SLOPE * x)
        col = edge_index[1]
        agg = jax.ops.segment_sum(edge_attr, col, num_segments=x.shape[0])
        h = jnp.concatenate([x, agg, u[batch]], axis=1)
        h = leaky_relu(h @ w1 + b1)
        h = leaky_relu(h @ w2 + b2)
        return h @ w3 + b3
    edge_index = jnp.stack([src, dst])
    batch0 = jnp.zeros((6250,), jnp.int32)
    h = jnp.maximum(_layernorm(x, axis=-1), 0.0)
    x = x + _L0_gnn_ref(h, edge_index, L0_gnn_W1, L0_gnn_b1, L0_gnn_W2, L0_gnn_b2)
    h = jnp.maximum(_layernorm(x, axis=-1), 0.0)
    x = x + _L1_gnn_ref(h, edge_index, edge_attr_64, L1_gnn_u, batch0, L1_gnn_w1, L1_gnn_b1, L1_gnn_w2, L1_gnn_b2, L1_gnn_w3, L1_gnn_b3)
    return x

_drawn_inputs = setup_inputs


def setup_inputs(seed=0):
    import zlib

    import numpy as np

    out = dict(_drawn_inputs(seed))
    spreads = {'L0_gnn_b1': (0.0, 0.579),
     'L0_gnn_b2': (0.0, 0.332),
     'L1_gnn_b1': (0.0, 0.652),
     'L1_gnn_b2': (0.0, 0.1),
     'L1_gnn_b3': (0.0, 0.1)}
    factors = {}
    for name, (base, spread) in spreads.items():
        noise = np.random.default_rng([zlib.crc32(name.encode()), seed]).standard_normal(out[name].shape)
        drawn = base * np.exp(spread * noise) if base else spread * noise
        out[name] = jnp.asarray(drawn.astype(out[name].dtype))
    for name, factor in factors.items():
        out[name] = (out[name] * factor).astype(out[name].dtype)
    return out
```

```python
from contextlib import ExitStack

import concourse.bass as bass
from concourse import mybir

ALU = mybir.AluOpType
ACT = mybir.ActivationFunctionType
AX = mybir.AxisListType
F32 = mybir.dt.float32
F16 = mybir.dt.float16
I32 = mybir.dt.int32

P = 128
N, F = 6250, 128
E = 206250
HI = -(-N // P)
NP = HI * P
TAIL = N - (HI - 1) * P

WN = 8
NW = NP // WN
WC = 3
WSLOTS = WC * P
MV = WN * HI
GW = 8
GN = GW * WN
NG = NW // GW
BG = 7
NB = NG // BG
BN = BG * GN
HG = HI // BG

AC = 19
ASLOTS = AC * P
EF = 64

EPR, EPC = 125, 1650
PADC = 1621
EP = E + P * PADC
SR = 512
NSR = -(-E // SR)
BIG = 8192.0
SC1 = 4096.0
TOP = 16384.0
EPS = 1e-5
ROUNDS = -(-E // WSLOTS) + 1


def build(nc, x, src, dst, attr, W1, b1, W2, b2, u, w1, c1, w2, c2, w3, c3, out):
    with ExitStack() as top:
        def sb(name, shape, dt, ctx=top):
            return ctx.enter_context(nc.sbuf_tensor(name, shape, dt))

        def ps(name, shape, ctx):
            return ctx.enter_context(nc.psum_tensor(name, shape, F32))

        def sem(name, ctx=top):
            return ctx.enter_context(nc.semaphore(name))

        def scratch(name, shape, dt):
            return nc.dram_tensor(name, shape, dt, kind="Internal").ap()

        ql_d = scratch("ql_d", (EP, 2), F32)
        dst_d = scratch("dst_d", (EP,), F32)
        first_d = scratch("first_d", (NP + P,), F32)
        win_d = scratch("win_d", (NW + WN,), F32)
        dis_d = scratch("dis_d", (NP,), F32)
        hT_d = scratch("hT_d", (F, NP), F32)
        h1T_d = scratch("h1T_d", (F, NP), F32)
        agg_d = scratch("agg_d", (EF, NP), F32)

        ident = sb("ident", [P, P], F32)
        ones = sb("ones", [1, P], F32)
        dis = sb("dis", [P, HI], F32)
        winf = sb("winf", [P, NW + WN], F32)
        win_i = sb("win_i", [1, NW], I32)
        rounds_i = sb("rounds_i", [1, 2], I32)
        iota_mv = sb("iota_mv", [P, MV], F16)
        iota_lo = sb("iota_lo", [P, P], F16)

        class Chain:

            def __init__(self, eng, s):
                self.eng, self.s, self.n = eng, s, 0

            def step(self, ins):
                self.n += 1
                ins.then_inc(self.s, 1)

            def wait(self):
                self.eng.wait_ge(self.s, self.n)

            def link(self, ins):
                self.step(ins)
                self.wait()

            def reuse(self, k, depth):
                if k >= depth:
                    self.eng.wait_ge(self.s, self.n - depth + 1)

        s_gate = sem("s_gate")

        def gate(eng, s, value):
            eng.wait_ge(s, value)
            eng.sem_inc(s_gate, 1)

        def inverse_root(ch, y, root, d, t):
            ch.link(nc.vector.reciprocal(y, root))
            ch.link(nc.vector.tensor_tensor(t, y, y, ALU.mult))
            ch.link(nc.vector.tensor_tensor(t, t, d, ALU.mult))
            ch.link(nc.vector.tensor_scalar(t, t, -0.5, 1.5, ALU.mult, ALU.add))
            ch.link(nc.vector.tensor_tensor(y, y, t, ALU.mult))

        with ExitStack() as ph:
            src_i = sb("src_i", [EPR, EPC], I32, ph)
            dst_i = sb("dst_i", [EPR, EPC], I32, ph)
            hi_i = sb("hi_i", [EPR, EPC], I32, ph)
            ql = sb("ql", [EPR, EPC, 2], F32, ph)
            dstf = sb("dstf", [EPR, EPC], F32, ph)
            qlpad = sb("qlpad", [P, PADC * 2], F32, ph)
            dstpad = sb("dstpad", [P, PADC], F32, ph)
            rel = sb("rel", [P, P], F32, ph)
            tgt = sb("tgt", [P, HI], F32, ph)
            heads = sb("heads", [1, NSR], F32, ph)
            heads_b = sb("heads_b", [P, NSR], F32, ph)
            rows = sb("rows", [P, HI, SR], F32, ph)
            cmp = sb("cmp", [P, 4, SR], F16, ph)
            cnt = sb("cnt", [P, HI], F32, ph)
            cnt2 = sb("cnt2", [P, HI], F32, ph)
            row_i = sb("row_i", [P, HI], I32, ph)
            firstT = sb("firstT", [HI, P], F32, ph)
            nextT = sb("nextT", [HI, P], F32, ph)
            disT = sb("disT", [HI, P], F32, ph)
            rootT = sb("rootT", [HI, P], F32, ph)
            tmpT = sb("tmpT", [HI, P], F32, ph)
            winT = sb("winT", [HI, P // WN], F32, ph)
            endc = sb("endc", [1, P], F32, ph)
            cap = sb("cap", [1, 2, ROUNDS], F32, ph)
            len_w = sb("len_w", [1, NW], F32, ph)
            len_g = sb("len_g", [1, NG], F32, ph)
            mx = sb("mx", [1, 2], F32, ph)
            rnd = sb("rnd", [1, 2], F32, ph)
            junk = sb("junk", [1, ROUNDS], F32, ph)
            heads_p = ps("heads_p", [P, 512], ph)
            firstT_p = ps("firstT_p", [HI, P], ph)
            dis_p = ps("dis_p", [P, HI], ph)

            s_edges = sem("s_edges", ph)
            s_iota = sem("s_iota", ph)
            s_codes = sem("s_codes", ph)
            s_pads = sem("s_pads", ph)
            s_stored = sem("s_stored", ph)
            s_heads = sem("s_heads", ph)
            s_heads_p = sem("s_heads_p", ph)
            s_rows_i = sem("s_rows_i", ph)
            s_rows = sem("s_rows", ph)
            s_first = sem("s_first", ph)
            s_firstT_p = sem("s_firstT_p", ph)
            s_firstT = sem("s_firstT", ph)
            s_first_d = sem("s_first_d", ph)
            s_next = sem("s_next", ph)
            s_root = sem("s_root", ph)
            s_var = sem("s_var", ph)
            s_disT = sem("s_disT", ph)
            s_dis_p = sem("s_dis_p", ph)
            s_dve = sem("s_dve", ph)

            block = ph.enter_context(nc.Block())

            @block.sync
            def _(sp):
                sp.dma_start(dst_i[:, :], dst.rearrange("(p c) -> p c", p=EPR)).then_inc(s_edges, 16)
                sp.dma_start(src_i[:, :], src.rearrange("(p c) -> p c", p=EPR)).then_inc(s_edges, 16)
                sp.wait_ge(s_codes, 1)
                sp.dma_start(dst_d[0:E].rearrange("(p c) -> p c", p=EPR), dstf[:, :]).then_inc(s_stored, 16)
                sp.wait_ge(s_pads, 2)
                sp.dma_start(dst_d[E:EP].rearrange("(p c) -> p c", p=P), dstpad[:, :]).then_inc(s_stored, 16)
                sp.wait_ge(s_stored, 32)
                with nc.allow_non_contiguous_dma(reason="one element of each row, once"):
                    sp.dma_start(heads[:, :], dst_d[0:NSR * SR].rearrange("(a r c) -> a r c", a=1, c=SR)[:, :, 0]
                                 ).then_inc(s_heads, 16)
                sp.wait_ge(s_codes, 2)
                sp.dma_start(ql_d[0:E, :].rearrange("(p c) t -> p (c t)", p=EPR),
                             ql[:, :, :].rearrange("p c t -> p (c t)")).then_inc(s_stored, 16)
                sp.dma_start(ql_d[E:EP, :].rearrange("(p c) t -> p (c t)", p=P), qlpad[:, :]).then_inc(s_stored, 16)
                sp.wait_ge(s_firstT, 1)
                sp.dma_start(first_d[0:NP].rearrange("(p c) -> p c", p=HI), firstT[:, :]).then_inc(s_first_d, 16)
                sp.dma_start(first_d[NP:NP + P].rearrange("(a c) -> a c", a=1), endc[:, :]).then_inc(s_first_d, 16)
                sp.dma_start(win_d[0:NW].rearrange("(p c) -> p c", p=HI), winT[:, :]).then_inc(s_first_d, 16)
                sp.dma_start(win_d[NW:NW + WN].rearrange("(a c) -> a c", a=1), endc[:, 0:WN]).then_inc(s_first_d, 16)
                sp.wait_ge(s_first_d, 64)
                sp.dma_start(nextT[:, :], first_d[1:NP + 1].rearrange("(p c) -> p c", p=HI)).then_inc(s_next, 16)
                sp.dma_start(winf[:, :], win_d.rearrange("(a c) -> a c", a=1).to_broadcast([P, NW + WN])
                             ).then_inc(s_next, 16)
                sp.wait_ge(s_disT, 1)
                sp.dma_start(dis_d.rearrange("(p c) -> p c", p=HI), rootT[:, :]).then_inc(s_stored, 16)
                sp.wait_ge(s_stored, 80)

            @block.gpsimd
            def _(pool):
                nc.gpsimd.iota(rel[:, :], [[1, P]], base=0, channel_multiplier=-1,
                               allow_small_or_imprecise_dtypes=True).then_inc(s_iota, 1)
                nc.gpsimd.iota(tgt[:, :], [[P, HI]], base=0, channel_multiplier=1,
                               allow_small_or_imprecise_dtypes=True).then_inc(s_iota, 1)
                nc.gpsimd.iota(iota_mv[:, :], [[1, MV]], base=0, channel_multiplier=0,
                               allow_small_or_imprecise_dtypes=True).then_inc(s_iota, 1)
                nc.gpsimd.iota(iota_lo[:, :], [[1, P]], base=0, channel_multiplier=0,
                               allow_small_or_imprecise_dtypes=True).then_inc(s_iota, 1)
                nc.gpsimd.memset(ones[:, :], 1.0).then_inc(s_iota, 1)
                nc.gpsimd.memset(dstpad[:, :], BIG).then_inc(s_pads, 1)
                nc.gpsimd.memset(qlpad[:, :], -1.0).then_inc(s_pads, 1)
                nc.gpsimd.iota(cap[:, 0, :], [[WSLOTS, ROUNDS]], base=0, channel_multiplier=0,
                               allow_small_or_imprecise_dtypes=True).then_inc(s_iota, 1)
                nc.gpsimd.iota(cap[:, 1, :], [[ASLOTS, ROUNDS]], base=0, channel_multiplier=0,
                               allow_small_or_imprecise_dtypes=True).then_inc(s_iota, 1)
                nc.gpsimd.memset(endc[:, :], float(E)).then_inc(s_iota, 1)
                pool.wait_ge(s_rows_i, 1)
                for k in range(HI):
                    nc.gpsimd.indirect_dma_start(
                        out=rows[:, k, :], out_offset=None,
                        in_=dst_d[0:NSR * SR].rearrange("(r c) -> r c", c=SR),
                        in_offset=bass.IndirectOffsetOnAxis(ap=row_i[:, k:k + 1], axis=0)).then_inc(s_rows, 16)

            @block.vector
            def _(dve):
                ch = Chain(dve, s_dve)
                dve.wait_ge(s_iota, 1)
                nc.vector.tensor_scalar(ident[:, :], rel[:, :], 0.0, None, ALU.is_equal)
                dve.wait_ge(s_edges, 32)
                nc.vector.tensor_copy(dstf[:, :], dst_i[:, :]).then_inc(s_codes, 1)
                ch.step(nc.vector.tensor_scalar(hi_i[:, :], src_i[:, :], 7, None, ALU.logical_shift_right))
                ch.link(nc.vector.tensor_scalar(src_i[:, :], src_i[:, :], P - 1, None, ALU.bitwise_and))
                ch.step(nc.vector.tensor_copy(ql[:, :, 1], src_i[:, :]))
                nc.vector.scalar_tensor_tensor(out=ql[:, :, 0], in0=dst_i[:, :], scalar=float(HI), in1=hi_i[:, :],
                                               op0=ALU.mult, op1=ALU.add).then_inc(s_codes, 1)
                dve.wait_ge(s_heads_p, 1)
                ch.link(nc.vector.tensor_copy(heads_b[:, :], heads_p[:, 0:NSR]))
                dve.wait_ge(s_iota, 2)
                for k in range(HI):
                    ch.reuse(k, 4)
                    ch.step(nc.vector.tensor_scalar(cmp[:, k % 4, 0:NSR], heads_b[:, :], tgt[:, k:k + 1], None,
                                                    ALU.is_lt, ALU.add, accum_out=cnt[:, k:k + 1]))
                ch.wait()
                ch.link(nc.vector.tensor_scalar(cnt[:, :], cnt[:, :], -1.0, 0.0, ALU.add, ALU.max))
                nc.vector.tensor_copy(row_i[:, :], cnt[:, :]).then_inc(s_rows_i, 1)
                dve.wait_ge(s_rows, 16 * HI)
                for k in range(HI):
                    ch.reuse(k, 4)
                    ch.step(nc.vector.tensor_scalar(cmp[:, k % 4, :], rows[:, k, :], tgt[:, k:k + 1], None,
                                                    ALU.is_lt, ALU.add, accum_out=cnt2[:, k:k + 1]))
                ch.wait()
                nc.vector.scalar_tensor_tensor(out=cnt[:, :], in0=cnt[:, :], scalar=float(SR), in1=cnt2[:, :],
                                               op0=ALU.mult, op1=ALU.add).then_inc(s_first, 1)
                dve.wait_ge(s_firstT_p, 1)
                ch.link(nc.vector.tensor_copy(firstT[:, :], firstT_p[:, :]))
                nc.vector.tensor_copy(winT[:, :], firstT[:, 0:P:WN]).then_inc(s_firstT, 1)
                dve.wait_ge(s_next, 32)
                ch.link(nc.vector.tensor_tensor(nextT[:, :], nextT[:, :], firstT[:, :], ALU.subtract))
                nc.vector.tensor_scalar(nextT[:, :], nextT[:, :], 1.0, 1.0, ALU.add, ALU.max).then_inc(s_var, 1)
                nc.vector.tensor_copy(win_i[:, :], winf[0:1, 0:NW])
                ch.step(nc.vector.tensor_tensor(len_w[:, :], winf[0:1, 1:NW + 1], winf[0:1, 0:NW], ALU.subtract))
                ch.link(nc.vector.tensor_tensor(len_g[:, :], winf[0:1, GW:NW + GW:GW], winf[0:1, 0:NW:GW],
                                                ALU.subtract))
                ch.step(nc.vector.tensor_reduce(mx[:, 0:1], len_w[:, :], AX.X, ALU.max))
                ch.link(nc.vector.tensor_reduce(mx[:, 1:2], len_g[:, :], AX.X, ALU.max))
                for k in range(2):
                    ch.link(nc.vector.tensor_scalar(junk[:, :], cap[:, k, :], mx[:, k:k + 1], None, ALU.is_lt,
                                                    ALU.add, accum_out=rnd[:, k:k + 1]))
                ch.link(nc.vector.tensor_copy(rounds_i[:, :], rnd[:, :]))
                dve.wait_ge(s_root, 1)
                inverse_root(ch, disT[:, :], rootT[:, :], nextT[:, :], tmpT[:, :])
                nc.vector.tensor_copy(rootT[:, :], disT[:, :]).then_inc(s_disT, 1)
                dve.wait_ge(s_dis_p, 1)
                ch.link(nc.vector.tensor_copy(dis[:, :], dis_p[:, :]))

            @block.scalar
            def _(act):
                act.wait_ge(s_var, 1)
                nc.scalar.activation(rootT[:, :], nextT[:, :], ACT.Sqrt).then_inc(s_root, 1)

            @block.tensor
            def _(pe):
                pe.wait_ge(s_iota, 8)
                pe.wait_ge(s_heads, 16)
                nc.tensor.matmul(heads_p[:, 0:NSR], ones[:, :], heads[:, :], start=True, stop=True
                                 ).then_inc(s_heads_p, 1)
                pe.wait_ge(s_first, 1)
                nc.tensor.transpose(firstT_p[:, :], cnt[:, :], ident[:, :]).then_inc(s_firstT_p, 1)
                pe.wait_ge(s_disT, 1)
                nc.tensor.transpose(dis_p[:, :], rootT[:, :], ident[0:HI, 0:HI]).then_inc(s_dis_p, 1)

        wcode = sb("wcode", [P, NW], F32)
        slots_ctx = top.enter_context(ExitStack())
        slots = sb("slots", [P, NW, WC, 2], F32, slots_ctx)

        def load_slots(eng, shift, s):
            with eng.Fori(0, NG) as i:
                for k in range(GW):
                    at = eng.value_load(win_i[0:1, bass.ds(i * GW + k, 1)], min_val=0, max_val=E)
                    eng.dma_start(slots[:, bass.ds(i * GW + k, 1), :, :].rearrange("p w c t -> p (w c t)"),
                                  ql_d[bass.ds(at + shift, WSLOTS), :].rearrange("(p c) t -> p (c t)", p=P)
                                  ).then_inc(s, 16)

        with ExitStack() as ph:
            rows = sb("arows", [P, 2, AC, EF], F32, ph)
            adst = sb("adst", [P, 2, AC], F32, ph)
            arel = sb("arel", [P, 2, 2, AC], F32, ph)
            hot = sb("ahot", [P, 2, AC, GN], F32, ph)
            agg = sb("agg", [EF, NP], F32, ph)
            pos = sb("pos", [P, AC], F32, ph)
            iota_n = sb("iota_n", [P, GN], F32, ph)
            gbase = sb("gbase", [P, NG], F32, ph)
            want = sb("want", [P, NG], F32, ph)
            over = sb("over", [P, NG], F32, ph)
            at_f = sb("at_f", [1, NG], F32, ph)
            at_i = sb("at_i", [1, NG], I32, ph)
            agg_p = [ps(f"agg_p{h}", [EF, GN], ph) for h in range(2)]

            s_const = sem("s_aconst", ph)
            s_off = sem("s_off", ph)
            s_loaded = [sem(f"s_loaded{h}", ph) for h in range(2)]
            s_hot = sem("s_hot", ph)
            s_summed = sem("s_summed", ph)
            s_slots = sem("s_slots", ph)
            s_slots_all = sem("s_slots_all", ph)
            s_agg_d = sem("s_agg_d", ph)
            s_done = sem("s_adone", ph)
            s_rel = sem("s_rel", ph)
            s_dve = sem("s_adve", ph)
            block = ph.enter_context(nc.Block())

            @block.gpsimd
            def _(pool):
                nc.gpsimd.iota(pos[:, :], [[1, AC]], base=0, channel_multiplier=AC,
                               allow_small_or_imprecise_dtypes=True).then_inc(s_const, 1)
                nc.gpsimd.iota(iota_n[:, :], [[1, GN]], base=0, channel_multiplier=0,
                               allow_small_or_imprecise_dtypes=True).then_inc(s_const, 1)
                nc.gpsimd.iota(gbase[:, :], [[-GN, NG]], base=0, channel_multiplier=0,
                               allow_small_or_imprecise_dtypes=True).then_inc(s_const, 1)
                nc.gpsimd.iota(wcode[:, :], [[MV, NW]], base=0, channel_multiplier=0,
                               allow_small_or_imprecise_dtypes=True).then_inc(s_const, 1)
                nc.gpsimd.memset(agg[:, :], 0.0).then_inc(s_const, 1)

            @block.sync
            def _(sp):
                rounds = sp.value_load(rounds_i[0:1, 1:2], min_val=1, max_val=ROUNDS)
                with sp.Fori(0, rounds) as r:
                    gate(sp, s_off, r + 1)
                    with sp.Fori(0, NG // 2) as i:
                        for h in range(2):
                            at = sp.value_load(at_i[0:1, bass.ds(2 * i + h, 1)], min_val=0, max_val=E - ASLOTS)
                            sp.wait_ge(s_summed, (r * (NG // 2) + i) * 2 + h + 1)
                            sp.dma_start(rows[:, h, :, :].rearrange("p c f -> p (c f)"),
                                         attr[bass.ds(at, ASLOTS), :].rearrange("(p c) f -> p (c f)", p=P)
                                         ).then_inc(s_loaded[h], 16)
                            sp.dma_start(adst[:, h, :],
                                         dst_d[bass.ds(at, ASLOTS)].rearrange("(p c) -> p c", p=P)
                                         ).then_inc(s_loaded[h], 16)
                sp.wait_ge(s_done, rounds)
                sp.dma_start(agg_d, agg[:, :]).then_inc(s_agg_d, 16)
                sp.wait_ge(s_agg_d, 16)

            @block.scalar
            def _(act):
                load_slots(act, 0, s_slots)
                act.wait_ge(s_slots, 16 * NW)
                act.sem_inc(s_slots_all, 1)

            @block.tensor
            def _(pe):
                rounds = pe.value_load(rounds_i[0:1, 1:2], min_val=1, max_val=ROUNDS)
                pe.sem_inc(s_summed, 2)
                with pe.Fori(0, rounds) as r:
                    with pe.Fori(0, NG // 2) as i:
                        for h in range(2):
                            pe.wait_ge(s_loaded[h], (r * (NG // 2) + i + 1) * 32)
                            pe.wait_ge(s_hot, (r * (NG // 2) + i) * 2 + h + 1)
                            for k in range(AC):
                                ins = nc.tensor.matmul(agg_p[h][:, :], rows[:, h, k, :], hot[:, h, k, :],
                                                       start=(k == 0), stop=(k == AC - 1))
                            ins.then_inc(s_summed, 1)

            @block.vector
            def _(dve):
                ch = Chain(dve, s_dve)
                dve.wait_ge(s_const, 5)
                ch.link(nc.vector.tensor_copy(want[:, :], winf[:, 0:NW:GW]))
                rounds = dve.value_load(rounds_i[0:1, 1:2], min_val=1, max_val=ROUNDS)
                with dve.Fori(0, rounds) as r:
                    nc.vector.tensor_scalar(at_f[:, :], want[0:1, :], float(E - ASLOTS), None, ALU.min
                                            ).then_inc(s_rel, 1)
                    dve.wait_ge(s_rel, r * (2 + NG) + 1)
                    nc.vector.tensor_copy(at_i[:, :], at_f[:, :]).then_inc(s_off, 1)
                    nc.vector.tensor_scalar(over[:, :], want[:, :], -float(E - ASLOTS), 0.0, ALU.add, ALU.max
                                            ).then_inc(s_rel, 1)
                    gate(dve, s_rel, r * (2 + NG) + 2)
                    with dve.Fori(0, NG // 2) as i:
                        for h in range(2):
                            n = (r * (NG // 2) + i) * 2 + h
                            g = 2 * i + h
                            dve.wait_ge(s_loaded[h], (r * (NG // 2) + i + 1) * 32)
                            dve.wait_ge(s_summed, n + 1)
                            nc.vector.tensor_scalar(arel[:, h, 0, :], pos[:, :], over[:, bass.ds(g, 1)], BIG,
                                                    ALU.is_lt, ALU.mult).then_inc(s_dve, 1)
                            dve.wait_ge(s_dve, 2 * n + 1 + 1)
                            nc.vector.scalar_tensor_tensor(out=arel[:, h, 1, :], in0=adst[:, h, :],
                                                           scalar=gbase[:, bass.ds(g, 1)], in1=arel[:, h, 0, :],
                                                           op0=ALU.add, op1=ALU.add).then_inc(s_dve, 1)
                            dve.wait_ge(s_dve, 2 * n + 2 + 1)
                            nc.vector.tensor_tensor(hot[:, h, :, :],
                                                    iota_n[:, :].unsqueeze(1).to_broadcast([P, AC, GN]),
                                                    arel[:, h, 1, :].unsqueeze(2).to_broadcast([P, AC, GN]),
                                                    ALU.is_equal).then_inc(s_hot, 1)
                            dve.wait_ge(s_summed, n + 1 + 2)
                            nc.vector.tensor_tensor(agg[:, bass.ds(g * GN, GN)], agg[:, bass.ds(g * GN, GN)],
                                                    agg_p[h][:, :], ALU.add).then_inc(s_rel, 1)
                    dve.wait_ge(s_rel, (r + 1) * (2 + NG))
                    nc.vector.tensor_scalar(want[:, :], want[:, :], float(ASLOTS), None, ALU.add
                                            ).then_inc(s_done, 1)
                    dve.wait_ge(s_done, r + 1)
                dve.wait_ge(s_slots_all, 1)
                nc.vector.tensor_tensor(slots[:, :, :, 0], slots[:, :, :, 0],
                                        wcode[:, :].unsqueeze(2).to_broadcast([P, NW, WC]), ALU.subtract)


        g_hi = sb("g_hi", [P, HI, F], F16)
        g_lo = sb("g_lo", [P, HI, F], F16)
        inv = sb("inv", [P, 1], F32)

        TB = 4
        BATCH = [(k, min(TB, HI - k)) for k in range(0, HI, TB)]

        def load_nodes(sp, tile, s):
            sp.dma_start(tile[:, 0:HI - 1, :], x[0:(HI - 1) * P, :].rearrange("(c p) f -> p c f", p=P)).then_inc(s, 16)
            sp.dma_start(tile[0:TAIL, HI - 1, :], x[(HI - 1) * P:N, :]).then_inc(s, 16)

        def layer_norm_relu(ch, act_root, v, t, m, r, w, y):
            def wide(a):
                return a[:, :].unsqueeze(2).to_broadcast([P, HI, F])
            ch.link(nc.vector.tensor_reduce(m[:, :], v[:, :, :], AX.X, ALU.add))
            ch.link(nc.vector.tensor_scalar(m[:, :], m[:, :], 1.0 / F, None, ALU.mult))
            ch.link(nc.vector.tensor_tensor(v[:, :, :], v[:, :, :], wide(m), ALU.subtract))
            ch.link(nc.vector.tensor_tensor(t[:, :, :], v[:, :, :], v[:, :, :], ALU.mult))
            ch.link(nc.vector.tensor_reduce(m[:, :], t[:, :, :], AX.X, ALU.add))
            ch.link(nc.vector.tensor_scalar(m[:, :], m[:, :], 1.0 / F, EPS, ALU.mult, ALU.add))
            act_root()
            inverse_root(ch, y[:, :], r[:, :], m[:, :], w[:, :])
            ch.link(nc.vector.tensor_tensor(v[:, :, :], v[:, :, :], wide(y), ALU.mult))
            ch.link(nc.vector.tensor_scalar(v[:, :, :], v[:, :, :], 0.0, None, ALU.max))

        with ExitStack() as ph:
            h = sb("h", [P, HI, F], F32, ph)
            t = sb("h_t", [P, HI, F], F32, ph)
            hT = sb("hT", [P, NP], F32, ph)
            m, r, w, y, sdis = (sb(f"ln1_{n}", [P, HI], F32, ph) for n in "mrwys")
            tp = ps("tp1", [P, 2, TB, P], ph)
            s_pad = sem("s_pad1", ph)
            s_x = sem("s_x1", ph)
            s_var = sem("s_var1", ph)
            s_root = sem("s_root1", ph)
            s_h = sem("s_h1", ph)
            s_turned = sem("s_turned1", ph)
            s_kept = sem("s_kept1", ph)
            s_hi = sem("s_hi1", ph)
            s_hT = sem("s_hT1", ph)
            s_dve = sem("s_dve1", ph)
            block = ph.enter_context(nc.Block())

            @block.sync
            def _(sp):
                sp.wait_ge(s_pad, 1)
                load_nodes(sp, h, s_x)
                sp.wait_ge(s_kept, len(BATCH))
                sp.dma_start(hT_d, hT[:, :]).then_inc(s_hT, 16)
                sp.wait_ge(s_hT, 16)

            @block.vector
            def _(dve):
                ch = Chain(dve, s_dve)
                nc.vector.memset(h[:, HI - 1, :], 0.0).then_inc(s_pad, 1)
                ch.link(nc.vector.memset(inv[:, :], 1.0 / SC1))
                dve.wait_ge(s_x, 32)

                def act_root():
                    ch.link(nc.vector.tensor_copy(w[:, :], m[:, :]))
                    dve.sem_inc(s_var, 1)
                    dve.wait_ge(s_root, 1)

                layer_norm_relu(ch, act_root, h, t, m, r, w, y)
                ch.link(nc.vector.tensor_scalar(sdis[:, :], dis[:, :], SC1, None, ALU.mult))
                nc.vector.tensor_tensor(t[:, :, :], h[:, :, :], sdis[:, :].unsqueeze(2).to_broadcast([P, HI, F]),
                                        ALU.mult).then_inc(s_h, 1)
                dve.wait_ge(s_hi, 1)
                ch.link(nc.vector.tensor_tensor(g_lo[:, :, :], t[:, :, :], g_hi[:, :, :], ALU.subtract))

            @block.scalar
            def _(act):
                act.wait_ge(s_var, 1)
                nc.scalar.activation(r[:, :], m[:, :], ACT.Sqrt).then_inc(s_root, 1)
                act.wait_ge(s_h, 1)
                nc.scalar.copy(g_hi[:, :, :], t[:, :, :]).then_inc(s_hi, 1)
                for i, (k, n) in enumerate(BATCH):
                    act.wait_ge(s_turned, i + 1)
                    nc.scalar.copy(hT[:, k * P:(k + n) * P], tp[:, i % 2, 0:n, :].rearrange("p n f -> p (n f)")
                                   ).then_inc(s_kept, 1)

            @block.tensor
            def _(pe):
                pe.wait_ge(s_h, 1)
                for i, (k, n) in enumerate(BATCH):
                    if i >= 2:
                        pe.wait_ge(s_kept, i - 1)
                    for c in range(n):
                        ins = nc.tensor.transpose(tp[:, i % 2, c, :], h[:, k + c, :], ident[:, :])
                    ins.then_inc(s_turned, 1)

        def aggregate(layer, total):
            with ExitStack() as ph:
                mv = sb(f"mv{layer}", [P, GW, WC, MV], F16, ph)
                st = sb(f"st{layer}", [P, GW, WC, P], F16, ph)
                adj = sb(f"adj{layer}", [P, 2, HI, BN], F16, ph)
                zeros = sb(f"zeros{layer}", [P, P], F16, ph)
                win_p = ps(f"win_p{layer}", [P, 4, 512], ph)
                dense_p = ps(f"dense_p{layer}", [P, 2, 512], ph)
                hot_ready = sem(f"hot_ready{layer}", ph)
                built = sem(f"built{layer}", ph)
                evicted = sem(f"evicted{layer}", ph)
                dense_done = sem(f"dense_done{layer}", ph)
                taken = sem(f"taken{layer}", ph)
                zeroed = sem(f"zeroed{layer}", ph)
                s_slots = sem(f"s_slots{layer}", ph)
                s_rel = sem(f"s_rel{layer}", ph)
                block = ph.enter_context(nc.Block())

                def load_rounds(eng):
                    return eng.value_load(rounds_i[0:1, 0:1], min_val=1, max_val=ROUNDS)

                @block.sync
                def _(sp):
                    rounds = load_rounds(sp)
                    with sp.Fori(0, rounds) as r:
                        with sp.If(rounds > 1):
                            gate(sp, dense_done, r * NB + 1)
                            load_slots(sp, r * WSLOTS, s_slots)

                @block.gpsimd
                def _(pool):
                    nc.gpsimd.memset(zeros[:, :], 0.0).then_inc(zeroed, 1)

                @block.vector
                def _(dve):
                    dve.sem_inc(taken, 2)
                    nc.vector.memset(total[:, :], 0.0).then_inc(zeroed, 1)
                    rounds = load_rounds(dve)

                    def group(r, i):
                        for k in range(GW):
                            dve.wait_ge(built, r * NW + i * GW + (k + 1))
                            for c in range(WC):
                                nc.vector.tensor_scalar(
                                    st[:, k, c, :], iota_lo[:, :],
                                    slots[:, bass.ds(i * GW + k, 1), c, 1], None, ALU.is_equal)
                                ins = nc.vector.tensor_scalar(
                                    mv[:, k, c, :], iota_mv[:, :],
                                    slots[:, bass.ds(i * GW + k, 1), c, 0], None, ALU.is_equal)
                            ins.then_inc(hot_ready, 1)

                    def add_block(r, b):
                        dve.wait_ge(dense_done, r * NB + b + 2)
                        nc.vector.tensor_tensor(
                            total[:, bass.ds(b * BN, BN)], total[:, bass.ds(b * BN, BN)],
                            dense_p[:, bass.ds(b % 2, 1), 0:BN].rearrange("p b n -> p (b n)"), ALU.add
                        ).then_inc(taken, 1)

                    gate(dve, zeroed, 2)
                    with dve.Fori(0, rounds) as r:
                        with dve.If(rounds > 1):
                            gate(dve, s_slots, (r + 1) * (16 * NW))
                            nc.vector.tensor_tensor(slots[:, :, :, 0], slots[:, :, :, 0],
                                                    wcode[:, :].unsqueeze(2).to_broadcast([P, NW, WC]),
                                                    ALU.subtract).then_inc(s_rel, 1)
                            gate(dve, s_rel, r + 1)
                        with dve.Fori(0, 2 * BG) as i:
                            group(r, i)
                        with dve.Fori(2, NB) as b:
                            group(r, b * BG)
                            add_block(r, b - 2)
                            with dve.Fori(1, BG) as j:
                                group(r, b * BG + j)
                        add_block(r, NB - 2)
                        add_block(r, NB - 1)

                @block.scalar
                def _(act):
                    act.sem_inc(evicted, 4)
                    rounds = load_rounds(act)
                    with act.Fori(0, rounds) as r:
                        with act.Fori(0, NB) as b:
                            with act.Fori(0, BG) as j:
                                for k in range(GW):
                                    gate(act, built, r * NW + b * (BG * GW) + j * GW + (GW + k + 1))
                                    nc.scalar.copy(
                                        adj[:, bass.ds(b % 2, 1), :, bass.ds(j * GN + k * WN, WN)]
                                        .rearrange("p b h d -> p d (b h)"),
                                        win_p[:, k % 4, 0:MV].rearrange("p (d h) -> p d h", d=WN)
                                    ).then_inc(evicted, 1)

                @block.tensor
                def _(pe):
                    pe.sem_inc(built, GW)
                    pe.sem_inc(dense_done, 1)
                    rounds = load_rounds(pe)

                    def build_window(r, i, k):
                        n = r * NW + i * GW + (k + 1)
                        pe.wait_ge(hot_ready, n)
                        pe.wait_ge(evicted, n)
                        for c in range(WC):
                            ins = nc.tensor.matmul(win_p[:, k % 4, 0:MV], st[:, k, c, :], mv[:, k, c, :],
                                                   start=(c == 0), stop=(c == WC - 1))
                        ins.then_inc(built, 1)

                    def bank(b):
                        return dense_p[:, bass.ds(b % 2, 1), 0:BN].rearrange("p b n -> p (b n)")

                    def open_block(r, b):
                        gate(pe, evicted, r * NW + b * (BG * GW) + (BG * GW + 4))
                        gate(pe, taken, r * NB + b + 1)
                        nc.tensor.matmul(bank(b), zeros[:, :], g_hi[:, 0:BN // P + 1, :].rearrange("p h f -> p (h f)")
                                         [:, 0:BN], start=True, stop=False)

                    def multiply(b, j, k):
                        part = adj[:, bass.ds(b % 2, 1), bass.ds(j * HG + k, 1), :].rearrange("p b h n -> p (b h n)")
                        for g in (g_hi, g_lo):
                            nc.tensor.matmul(bank(b), g[:, bass.ds(j * HG + k, 1), :].rearrange("p h f -> p (h f)"),
                                             part, start=False, stop=False)

                    def close_block(b):
                        nc.tensor.matmul(bank(b), zeros[:, :], g_hi[:, 0:BN // P + 1, :].rearrange("p h f -> p (h f)")
                                         [:, 0:BN], start=False, stop=True).then_inc(dense_done, 1)

                    gate(pe, zeroed, 2)
                    with pe.Fori(0, rounds) as r:
                        with pe.Fori(0, BG) as j:
                            for k in range(GW):
                                build_window(r, j, k)
                        with pe.Fori(1, NB) as b:
                            open_block(r, b - 1)
                            with pe.Fori(0, BG) as j:
                                for k in range(GW):
                                    build_window(r, b * BG + j, k)
                                    if k < HG:
                                        multiply(b - 1, j, k)
                            close_block(b - 1)
                        open_block(r, NB - 1)
                        with pe.Fori(0, BG) as j:
                            for k in range(HG):
                                multiply(NB - 1, j, k)
                        close_block(NB - 1)

        def after_aggregate(layer, total, W, b):
            with ExitStack() as ph:
                cur = sb(f"cur{layer}", [P, NP], F32, ph)
                disb = sb(f"disb{layer}", [P, NP], F32, ph)
                hn = sb(f"hn{layer}", [P, NP], F32, ph)
                W_sb = sb(f"W_sb{layer}", [P, F], F32, ph)
                b_sb = sb(f"b_sb{layer}", [P, 1], F32, ph)
                mx = sb(f"mx{layer}", [P, NB], F32, ph)
                m1 = sb(f"m1{layer}", [P, 1], F32, ph)
                sdis = sb(f"sdis{layer}", [P, HI], F32, ph)
                node = sb(f"node{layer}", [P, HI, F], F32, ph)
                if layer == 2:
                    h0 = sb("h0", [P, NP], F32, ph)
                lin_p = ps(f"lin_p{layer}", [P, 2, 512], ph)
                tp = ps(f"tp_l{layer}", [P, 2, TB, P], ph)
                s_cur = sem(f"s_cur{layer}", ph)
                s_w = sem(f"s_w{layer}", ph)
                s_x = sem(f"s_x_l{layer}", ph)
                s_pad = sem(f"s_pad_l{layer}", ph)
                s_mixed = sem(f"s_mixed{layer}", ph)
                s_lin = sem(f"s_lin{layer}", ph)
                s_hn = sem(f"s_hn{layer}", ph)
                s_comb = sem(f"s_comb{layer}", ph)
                s_max = sem(f"s_max{layer}", ph)
                s_all = sem(f"s_all{layer}", ph)
                s_turned = sem(f"s_turned_l{layer}", ph)
                s_node = sem(f"s_node{layer}", ph)
                s_hi = sem(f"s_hi{layer}b", ph)
                s_out = sem(f"s_out{layer}", ph)
                s_dve = sem(f"s_dve_l{layer}", ph)
                block = ph.enter_context(nc.Block())

                @block.sync
                def _(sp):
                    sp.dma_start(disb[:, :], dis_d.rearrange("(a n) -> a n", a=1).to_broadcast([P, NP])
                                 ).then_inc(s_cur, 16)
                    sp.dma_start(cur[:, :], hT_d if layer == 1 else h1T_d).then_inc(s_cur, 16)
                    sp.dma_start(W_sb[:, :], W).then_inc(s_w, 16)
                    with nc.allow_non_contiguous_dma(reason="a bias, one element per partition"):
                        sp.dma_start(b_sb[:, :], b.rearrange("(p a) -> p a", a=1)).then_inc(s_w, 16)
                    if layer == 2:
                        sp.dma_start(h0[:, :], hT_d).then_inc(s_x, 16)
                        sp.wait_ge(s_pad, 1)
                        load_nodes(sp, node, s_x)
                        sp.wait_ge(s_node, len(BATCH))
                        sp.dma_start(x1_d, node[:, :, :].rearrange("p c f -> p (c f)")).then_inc(s_out, 16)
                    else:
                        sp.wait_ge(s_hn, NB)
                        sp.dma_start(h1T_d, hn[:, :]).then_inc(s_out, 16)
                    sp.wait_ge(s_out, 16)

                @block.gpsimd
                def _(pool):
                    if layer == 1:
                        pool.wait_ge(s_max, 1)
                        nc.gpsimd.partition_all_reduce(m1[:, :], m1[:, :], P, bass.bass_isa.ReduceOp.max
                                                       ).then_inc(s_all, 1)

                @block.vector
                def _(dve):
                    ch = Chain(dve, s_dve)
                    if layer == 2:
                        nc.vector.memset(node[:, HI - 1, :], 0.0).then_inc(s_pad, 1)
                    dve.wait_ge(s_cur, 32)
                    for c in range(NB):
                        cols = slice(c * BN, (c + 1) * BN)
                        ch.link(nc.vector.tensor_tensor(cur[:, cols], cur[:, cols], disb[:, cols], ALU.mult))
                        ch.link(nc.vector.scalar_tensor_tensor(out=total[:, cols], in0=total[:, cols],
                                                               scalar=inv[:, 0:1], in1=cur[:, cols],
                                                               op0=ALU.mult, op1=ALU.add))
                        nc.vector.tensor_tensor(total[:, cols], total[:, cols], disb[:, cols], ALU.mult
                                                ).then_inc(s_mixed, 1)
                    if layer == 1:
                        for c in range(NB):
                            dve.wait_ge(s_hn, c + 1)
                            ch.step(nc.vector.tensor_reduce(mx[:, c:c + 1], hn[:, c * BN:(c + 1) * BN], AX.X, ALU.max))
                        ch.wait()
                        nc.vector.tensor_reduce(m1[:, :], mx[:, :], AX.X, ALU.max).then_inc(s_max, 1)
                        dve.wait_ge(s_all, 1)
                        ch.link(nc.vector.tensor_scalar(m1[:, :], m1[:, :], 1.0 / TOP, 1e-30, ALU.mult, ALU.max))
                        ch.link(nc.vector.tensor_copy(inv[:, :], m1[:, :]))
                        ch.link(nc.vector.reciprocal(mx[:, 0:1], m1[:, :]))
                        ch.link(nc.vector.tensor_scalar(sdis[:, :], dis[:, :], mx[:, 0:1], None, ALU.mult))
                        for i, (k, n) in enumerate(BATCH):
                            dve.wait_ge(s_turned, i + 1)
                            nc.vector.tensor_tensor(node[:, k:k + n, :], tp[:, i % 2, 0:n, :],
                                                    sdis[:, k:k + n].unsqueeze(2).to_broadcast([P, n, F]),
                                                    ALU.mult).then_inc(s_node, 1)
                        for i, (k, n) in enumerate(BATCH):
                            dve.wait_ge(s_hi, i + 1)
                            nc.vector.tensor_tensor(g_lo[:, k:k + n, :], node[:, k:k + n, :], g_hi[:, k:k + n, :],
                                                    ALU.subtract)
                    else:
                        dve.wait_ge(s_x, 48)
                        for c in range(NB):
                            cols = slice(c * BN, (c + 1) * BN)
                            dve.wait_ge(s_hn, c + 1)
                            ch.link(nc.vector.tensor_tensor(hn[:, cols], hn[:, cols], h0[:, cols], ALU.add))
                            nc.vector.tensor_scalar(hn[:, cols], hn[:, cols], 0.5, None, ALU.mult).then_inc(s_comb, 1)
                        for i, (k, n) in enumerate(BATCH):
                            dve.wait_ge(s_turned, i + 1)
                            nc.vector.tensor_tensor(node[:, k:k + n, :], node[:, k:k + n, :], tp[:, i % 2, 0:n, :],
                                                    ALU.add).then_inc(s_node, 1)

                @block.scalar
                def _(act):
                    act.wait_ge(s_w, 32)
                    for c in range(NB):
                        act.wait_ge(s_lin, c + 1)
                        nc.scalar.activation(hn[:, c * BN:(c + 1) * BN], lin_p[:, c % 2, 0:BN], ACT.Relu,
                                             bias=b_sb[:, 0:1]).then_inc(s_hn, 1)
                    if layer == 1:
                        for i, (k, n) in enumerate(BATCH):
                            act.wait_ge(s_node, i + 1)
                            nc.scalar.copy(g_hi[:, k:k + n, :], node[:, k:k + n, :]).then_inc(s_hi, 1)

                @block.tensor
                def _(pe):
                    pe.wait_ge(s_w, 32)
                    for c in range(NB):
                        pe.wait_ge(s_mixed, c + 1)
                        if c >= 2:
                            pe.wait_ge(s_hn, c - 1)
                        nc.tensor.matmul(lin_p[:, c % 2, 0:BN], W_sb[:, :], total[:, c * BN:(c + 1) * BN],
                                         start=True, stop=True).then_inc(s_lin, 1)
                    pe.wait_ge(s_comb if layer == 2 else s_hn, NB)
                    for i, (k, n) in enumerate(BATCH):
                        if i >= 2:
                            pe.wait_ge(s_node, i - 1)
                        for c in range(n):
                            ins = nc.tensor.transpose(tp[:, i % 2, c, :], hn[:, (k + c) * P:(k + c + 1) * P],
                                                      ident[:, :])
                        ins.then_inc(s_turned, 1)

        def mlp():
            M1, M2 = w1.shape[1] // P, w2.shape[1] // P
            KU = F + EF
            SLOPE = 0.01
            CH = [(k, min(TB, HI - k)) for k in range(0, HI, TB)]
            with ExitStack() as ph:
                x1 = sb("x1", [P, HI, F], F32, ph)
                h = sb("hm", [P, HI, F], F32, ph)
                t = sb("tm", [P, HI, F], F32, ph)
                m, r, w, y = (sb(f"ln2_{n}", [P, HI], F32, ph) for n in "mrwy")
                agg = sb("agg_m", [EF, NP], F32, ph)
                w1a = sb("w1a", [P, M1 * P], F32, ph)
                w1b = sb("w1b", [EF, M1 * P], F32, ph)
                w1u = sb("w1u", [EF, M1 * P], F32, ph)
                w2_sb = sb("w2_sb", [P, M1, M2 * P], F32, ph)
                w3_sb = sb("w3_sb", [P, M2, F], F32, ph)
                u_sb = sb("u_sb", [EF, 1], F32, ph)
                c1_sb = sb("c1_sb", [P, M1], F32, ph)
                c2_sb = sb("c2_sb", [P, M2], F32, ph)
                c3_sb = sb("c3_sb", [1, F], F32, ph)
                hT = sb("hmT", [P, 2, TB * P], F32, ph)
                z1 = sb("z1", [P, 2, M1, TB * P], F32, ph)
                a1 = sb("a1", [P, 2, M1, TB * P], F32, ph)
                z2 = sb("z2", [P, 2, M2, TB * P], F32, ph)
                a2 = sb("a2", [P, 2, M2, TB * P], F32, ph)
                tp = ps("tpm", [P, TB * P], ph)
                z1_p = ps("z1_p", [P, M1, 512], ph)
                z2_p = ps("z2_p", [P, M2, 512], ph)
                y_p = ps("y_p", [P, 2, TB, F], ph)
                uc_p = ps("uc_p", [P, M1], ph)
                s_x = sem("s_xm", ph)
                s_w = sem("s_wm", ph)
                s_var = sem("s_varm", ph)
                s_root = sem("s_rootm", ph)
                s_h = sem("s_hm", ph)
                s_uc = sem("s_uc", ph)
                s_c1 = sem("s_c1", ph)
                s_turned = sem("s_turnedm", ph)
                s_hT = sem("s_hTm", ph)
                s_z1p = sem("s_z1p", ph)
                s_z1 = sem("s_z1", ph)
                s_a1 = sem("s_a1", ph)
                s_z2p = sem("s_z2p", ph)
                s_z2 = sem("s_z2", ph)
                s_a2 = sem("s_a2", ph)
                s_yp = sem("s_yp", ph)
                s_y = sem("s_y", ph)
                s_out = sem("s_outm", ph)
                s_dve = sem("s_dvem", ph)
                block = ph.enter_context(nc.Block())

                @block.sync
                def _(sp):
                    sp.dma_start(x1[:, :, :].rearrange("p c f -> p (c f)"), x1_d).then_inc(s_x, 16)
                    sp.dma_start(h[:, :, :].rearrange("p c f -> p (c f)"), x1_d).then_inc(s_x, 16)
                    sp.dma_start(agg[:, :], agg_d).then_inc(s_w, 16)
                    sp.dma_start(w1a[:, :], w1[0:F, :]).then_inc(s_w, 16)
                    sp.dma_start(w1b[:, :], w1[F:KU, :]).then_inc(s_w, 16)
                    sp.dma_start(w1u[:, :], w1[KU:KU + EF, :]).then_inc(s_w, 16)
                    sp.dma_start(w2_sb[:, :, :], w2.rearrange("(m p) n -> p m n", p=P)).then_inc(s_w, 16)
                    sp.dma_start(w3_sb[:, :, :], w3.rearrange("(m p) n -> p m n", p=P)).then_inc(s_w, 16)
                    sp.dma_start(c3_sb[:, :], c3.rearrange("(a n) -> a n", a=1)).then_inc(s_w, 16)
                    with nc.allow_non_contiguous_dma(reason="biases, one element per partition"):
                        sp.dma_start(u_sb[:, :], u[0:1, :].rearrange("a n -> n a")).then_inc(s_w, 16)
                        sp.dma_start(c1_sb[:, :], c1.rearrange("(m p) -> p m", p=P)).then_inc(s_w, 16)
                        sp.dma_start(c2_sb[:, :], c2.rearrange("(m p) -> p m", p=P)).then_inc(s_w, 16)
                    for i, (k, n) in enumerate(CH):
                        sp.wait_ge(s_y, i + 1)
                        full = n if k + n < HI else n - 1
                        if full:
                            sp.dma_start(out[k * P:(k + full) * P, :].rearrange("(c p) f -> p c f", p=P),
                                         x1[:, k:k + full, :]).then_inc(s_out, 16)
                        if full < n:
                            sp.dma_start(out[(HI - 1) * P:N, :], x1[0:TAIL, HI - 1, :]).then_inc(s_out, 16)
                    outs = len(CH) + (1 if CH[-1][1] > 1 else 0)
                    sp.wait_ge(s_out, 16 * outs)

                @block.vector
                def _(dve):
                    ch = Chain(dve, s_dve)
                    dve.wait_ge(s_x, 32)

                    def act_root():
                        ch.link(nc.vector.tensor_copy(w[:, :], m[:, :]))
                        dve.sem_inc(s_var, 1)
                        dve.wait_ge(s_root, 1)

                    layer_norm_relu(ch, act_root, h, t, m, r, w, y)
                    dve.sem_inc(s_h, 1)
                    dve.wait_ge(s_w, 160)
                    dve.wait_ge(s_uc, 1)
                    nc.vector.tensor_tensor(c1_sb[:, :], c1_sb[:, :], uc_p[:, :], ALU.add).then_inc(s_c1, 1)

                    def leaky(i, n, z, a, s_in, s_done):
                        dve.wait_ge(s_in, i + 1)
                        nc.vector.scalar_tensor_tensor(out=a[:, i % 2, :, 0:n * P], in0=z[:, i % 2, :, 0:n * P],
                                                       scalar=SLOPE, in1=z[:, i % 2, :, 0:n * P],
                                                       op0=ALU.mult, op1=ALU.max).then_inc(s_done, 1)

                    for i, (k, n) in enumerate(CH):
                        dve.wait_ge(s_turned, i + 1)
                        if i >= 2:
                            dve.wait_ge(s_z1p, i - 1)
                        nc.vector.tensor_copy(hT[:, i % 2, 0:n * P], tp[:, 0:n * P]).then_inc(s_hT, 1)
                        if i >= 2:
                            dve.wait_ge(s_z2p, i - 1)
                        leaky(i, n, z1, a1, s_z1, s_a1)
                        if i >= 2:
                            dve.wait_ge(s_yp, i - 1)
                        leaky(i, n, z2, a2, s_z2, s_a2)
                        dve.wait_ge(s_yp, i + 1)
                        nc.vector.tensor_tensor(x1[:, k:k + n, :], x1[:, k:k + n, :], y_p[:, i % 2, 0:n, :], ALU.add
                                                ).then_inc(s_y, 1)

                @block.scalar
                def _(act):
                    act.wait_ge(s_var, 1)
                    nc.scalar.activation(r[:, :], m[:, :], ACT.Sqrt).then_inc(s_root, 1)
                    act.wait_ge(s_c1, 1)
                    for i, (k, n) in enumerate(CH):
                        act.wait_ge(s_z1p, i + 1)
                        if i >= 2:
                            act.wait_ge(s_a1, i - 1)
                        for q in range(M1):
                            ins = nc.scalar.activation(z1[:, i % 2, q, 0:n * P], z1_p[:, q, 0:n * P], ACT.Identity,
                                                       bias=c1_sb[:, q:q + 1])
                        ins.then_inc(s_z1, 1)
                        act.wait_ge(s_z2p, i + 1)
                        if i >= 2:
                            act.wait_ge(s_a2, i - 1)
                        for q in range(M2):
                            ins = nc.scalar.activation(z2[:, i % 2, q, 0:n * P], z2_p[:, q, 0:n * P], ACT.Identity,
                                                       bias=c2_sb[:, q:q + 1])
                        ins.then_inc(s_z2, 1)

                @block.tensor
                def _(pe):
                    pe.wait_ge(s_w, 160)
                    for q in range(M1):
                        ins = nc.tensor.matmul(uc_p[:, q:q + 1], w1u[:, q * P:(q + 1) * P], u_sb[:, :],
                                               start=True, stop=True)
                    ins.then_inc(s_uc, 1)
                    pe.wait_ge(s_h, 1)
                    for i, (k, n) in enumerate(CH):
                        if i >= 1:
                            pe.wait_ge(s_hT, i)
                        for c in range(n):
                            ins = nc.tensor.transpose(tp[:, c * P:(c + 1) * P], h[:, k + c, :], ident[:, :])
                        ins.then_inc(s_turned, 1)
                        pe.wait_ge(s_hT, i + 1)
                        if i >= 1:
                            pe.wait_ge(s_z1, i)
                        for q in range(M1):
                            nc.tensor.matmul(z1_p[:, q, 0:n * P], w1a[:, q * P:(q + 1) * P], hT[:, i % 2, 0:n * P],
                                             start=True, stop=False)
                            ins = nc.tensor.matmul(z1_p[:, q, 0:n * P], w1b[:, q * P:(q + 1) * P],
                                                   agg[:, k * P:(k + n) * P], start=False, stop=True)
                        ins.then_inc(s_z1p, 1)
                        pe.wait_ge(s_a1, i + 1)
                        if i >= 1:
                            pe.wait_ge(s_z2, i)
                        for q in range(M2):
                            for c in range(M1):
                                ins = nc.tensor.matmul(z2_p[:, q, 0:n * P], w2_sb[:, c, q * P:(q + 1) * P],
                                                       a1[:, i % 2, c, 0:n * P], start=(c == 0), stop=(c == M1 - 1))
                        ins.then_inc(s_z2p, 1)
                        pe.wait_ge(s_a2, i + 1)
                        if i >= 2:
                            pe.wait_ge(s_y, i - 1)
                        for v in range(n):
                            nc.tensor.matmul(y_p[:, i % 2, v, :], ones[:, :], c3_sb[:, :], start=True, stop=False)
                            for c in range(M2):
                                ins = nc.tensor.matmul(y_p[:, i % 2, v, :], a2[:, i % 2, c, v * P:(v + 1) * P],
                                                       w3_sb[:, c, :], start=False, stop=(c == M2 - 1))
                        ins.then_inc(s_yp, 1)

        x1_d = scratch("x1_d", (P, HI * F), F32)
        with ExitStack() as ly:
            total = sb("total", [P, NP], F32, ly)
            aggregate(1, total)
            after_aggregate(1, total, W1, b1)
            aggregate(2, total)
            after_aggregate(2, total, W2, b2)
        mlp()


_INS = ['x', 'src', 'dst', 'edge_attr_64', 'L0_gnn_W1', 'L0_gnn_b1', 'L0_gnn_W2', 'L0_gnn_b2', 'L1_gnn_u',
        'L1_gnn_w1', 'L1_gnn_b1', 'L1_gnn_w2', 'L1_gnn_b2', 'L1_gnn_w3', 'L1_gnn_b3']


def kernel(**inputs):
    import numpy as _np
    import concourse.bacc as _bacc
    from concourse import mybir as _mybir
    from concourse.bass_utils import run_bass_kernel_spmd as _run

    nc = _bacc.Bacc("TRN2", target_bir_lowering=False, num_devices=1)
    arrays, args = {}, []
    for name in _INS:
        a = _np.ascontiguousarray(inputs[name])
        arrays[f"in_{name}_dram"] = a
        args.append(nc.dram_tensor(f"in_{name}_dram", a.shape, _mybir.dt.from_np(a.dtype), kind="ExternalInput").ap())
    out = nc.dram_tensor("out_0_dram", (6250, 128), _mybir.dt.float32, kind="ExternalOutput").ap()
    build(nc, *args, out)
    r = _run(nc, [arrays], core_ids=[0])
    return r.results[0]["out_0_dram"]
```

```python
from contextlib import ExitStack

import concourse.bass as bass
from concourse import mybir

ALU = mybir.AluOpType
ACT = mybir.ActivationFunctionType
AX = mybir.AxisListType
F32 = mybir.dt.float32
F16 = mybir.dt.float16
I32 = mybir.dt.int32
I16 = mybir.dt.int16

P = 128
N, F = 6250, 128
E = 206250
HI = -(-N // P)
NP = HI * P
TAIL = N - (HI - 1) * P

WN = 8
NW = NP // WN
WC = 3
WSLOTS = WC * P
MV = WN * HI
GW = 8
GN = GW * WN
NG = NW // GW
BG = 7
NB = NG // BG
BN = BG * GN
HG = HI // BG

AC = 19
ASLOTS = AC * P
EF = 64

EPR, EPC = 125, 1650
PADC = 1622
EP = E + P * PADC
SB = 7
SR = 512
NSR = -(-E // SR)
BIG = 8192.0
SC1 = 4096.0
TOP = 16384.0
EPS = 1e-5
ROUNDS = -(-E // WSLOTS) + 1


def build(nc, x, src, dst, attr, W1, b1, W2, b2, u, w1, c1, w2, c2, w3, c3, out):
    with ExitStack() as top:
        def sb(name, shape, dt, ctx=top):
            return ctx.enter_context(nc.sbuf_tensor(name, shape, dt))

        def ps(name, shape, ctx):
            return ctx.enter_context(nc.psum_tensor(name, shape, F32))

        def sem(name, ctx=top):
            return ctx.enter_context(nc.semaphore(name))

        def scratch(name, shape, dt):
            return nc.dram_tensor(name, shape, dt, kind="Internal").ap()

        ql_d = scratch("ql_d", (EP, 2), F32)
        dst_d = scratch("dst_d", (EP,), I16)
        first_d = scratch("first_d", (NP + P,), F32)
        win_d = scratch("win_d", (NW + WN,), F32)
        dis_d = scratch("dis_d", (NP,), F32)
        hT_d = scratch("hT_d", (F, NP), F32)
        h1T_d = scratch("h1T_d", (F, NP), F32)
        adj_d = scratch("adj_d", (P, HI, NP), F16)
        agg_d = scratch("agg_d", (EF, NP), F32)

        ident = sb("ident", [P, P], F32)
        ones = sb("ones", [1, P], F32)
        dis = sb("dis", [P, HI], F32)
        winf = sb("winf", [P, NW + WN], F32)
        win_i = sb("win_i", [1, NW], I32)
        rounds_i = sb("rounds_i", [1, 2], I32)
        iota_mv = sb("iota_mv", [P, MV], F16)
        iota_lo = sb("iota_lo", [P, P, WC], F16)
        wcode = sb("wcode", [P, NW], F32)
        g_hi = sb("g_hi", [P, HI, F], F16)
        g_lo = sb("g_lo", [P, HI, F], F16)
        inv = sb("inv", [P, 1], F32)

        class Chain:

            def __init__(self, eng, s):
                self.eng, self.s, self.n = eng, s, 0

            def step(self, ins):
                self.n += 1
                ins.then_inc(self.s, 1)

            def wait(self):
                self.eng.wait_ge(self.s, self.n)

            def link(self, ins):
                self.step(ins)
                self.wait()

            def reuse(self, k, depth):
                if k >= depth:
                    self.eng.wait_ge(self.s, self.n - depth + 1)

        s_gate = sem("s_gate")

        def gate(eng, s, value):
            eng.wait_ge(s, value)
            eng.sem_inc(s_gate, 1)

        def inverse_root(ch, y, root, d, t):
            ch.link(nc.vector.reciprocal(y, root))
            ch.link(nc.vector.tensor_tensor(t, y, y, ALU.mult))
            ch.link(nc.vector.tensor_tensor(t, t, d, ALU.mult))
            ch.link(nc.vector.tensor_scalar(t, t, -0.5, 1.5, ALU.mult, ALU.add))
            ch.link(nc.vector.tensor_tensor(y, y, t, ALU.mult))

        TB = 4
        BATCH = [(k, min(TB, HI - k)) for k in range(0, HI, TB)]

        def load_nodes(sp, tile, s):
            sp.dma_start(tile[:, 0:HI - 1, :], x[0:(HI - 1) * P, :].rearrange("(c p) f -> p c f", p=P)).then_inc(s, 16)
            sp.dma_start(tile[0:TAIL, HI - 1, :], x[(HI - 1) * P:N, :]).then_inc(s, 16)

        def layer_norm_relu(ch, act_root, v, t, m, r, w, y):
            def wide(a):
                return a[:, :].unsqueeze(2).to_broadcast([P, HI, F])
            ch.link(nc.vector.tensor_reduce(m[:, :], v[:, :, :], AX.X, ALU.add))
            ch.link(nc.vector.tensor_scalar(m[:, :], m[:, :], 1.0 / F, None, ALU.mult))
            ch.link(nc.vector.tensor_tensor(v[:, :, :], v[:, :, :], wide(m), ALU.subtract))
            ch.link(nc.vector.tensor_tensor(t[:, :, :], v[:, :, :], v[:, :, :], ALU.mult))
            ch.link(nc.vector.tensor_reduce(m[:, :], t[:, :, :], AX.X, ALU.add))
            ch.link(nc.vector.tensor_scalar(m[:, :], m[:, :], 1.0 / F, EPS, ALU.mult, ALU.add))
            act_root()
            inverse_root(ch, y[:, :], r[:, :], m[:, :], w[:, :])
            ch.link(nc.vector.tensor_tensor(v[:, :, :], v[:, :, :], wide(y), ALU.mult))
            ch.link(nc.vector.tensor_scalar(v[:, :, :], v[:, :, :], 0.0, None, ALU.max))

        operand_ctx = top.enter_context(ExitStack())
        h = sb("h", [P, HI, F], F32, operand_ctx)
        t = sb("h_t", [P, HI, F], F32, operand_ctx)

        with ExitStack() as ph:
            src_i = sb("src_i", [EPR, EPC], I32, ph)
            dst_i = sb("dst_i", [EPR, EPC], I32, ph)
            hi_i = sb("hi_i", [EPR, EPC], I32, ph)
            ql = sb("ql", [EPR, EPC, 2], F32, ph)
            dst16 = sb("dst16", [EPR, EPC], I16, ph)
            qlpad = sb("qlpad", [P, PADC], F32, ph)
            dstpad = sb("dstpad", [P, PADC], I16, ph)
            rel = sb("rel", [P, P], F32, ph)
            tgt = sb("tgt", [P, HI], F32, ph)
            heads_i = sb("heads_i", [1, NSR], I16, ph)
            heads = sb("heads", [1, NSR], F32, ph)
            heads_b = sb("heads_b", [P, NSR], F32, ph)
            rows = sb("rows", [P, HI, SR], I16, ph)
            cmp = sb("cmp", [P, 4, SR], F16, ph)
            cnt = sb("cnt", [P, HI], F32, ph)
            cnt2 = sb("cnt2", [P, HI], F32, ph)
            row_i = sb("row_i", [P, HI], I32, ph)
            firstT = sb("firstT", [HI, P], F32, ph)
            nextT = sb("nextT", [HI, P], F32, ph)
            disT = sb("disT", [HI, P], F32, ph)
            rootT = sb("rootT", [HI, P], F32, ph)
            tmpT = sb("tmpT", [HI, P], F32, ph)
            winT = sb("winT", [HI, P // WN], F32, ph)
            endc = sb("endc", [1, P], F32, ph)
            cap = sb("cap", [1, 2, ROUNDS], F32, ph)
            len_w = sb("len_w", [1, NW], F32, ph)
            len_g = sb("len_g", [1, NG], F32, ph)
            mx = sb("mx", [1, 2], F32, ph)
            rnd = sb("rnd", [1, 2], F32, ph)
            m, r, w, y = (sb(f"ln1_{n}", [P, HI], F32, ph) for n in "mrwy")
            heads_p = ps("heads_p", [P, 512], ph)
            firstT_p = ps("firstT_p", [HI, P], ph)
            dis_p = ps("dis_p", [P, HI], ph)

            s_edges = sem("s_edges", ph)
            s_iota = sem("s_iota", ph)
            s_codes = sem("s_codes", ph)
            s_pads = sem("s_pads", ph)
            s_stored = sem("s_stored", ph)
            s_heads = sem("s_heads", ph)
            s_heads_p = sem("s_heads_p", ph)
            s_rows_i = sem("s_rows_i", ph)
            s_rows = [sem(f"s_rows{b}", ph) for b in range(HI // SB)]
            s_first = sem("s_first", ph)
            s_firstT_p = sem("s_firstT_p", ph)
            s_firstT = sem("s_firstT", ph)
            s_first_d = sem("s_first_d", ph)
            s_next = sem("s_next", ph)
            s_root = sem("s_root", ph)
            s_var = sem("s_var", ph)
            s_disT = sem("s_disT", ph)
            s_dis_p = sem("s_dis_p", ph)
            s_dve = sem("s_dve", ph)
            s_pad = sem("s_pad1", ph)
            s_x = sem("s_x1", ph)
            s_lnvar = sem("s_lnvar", ph)
            s_lnroot = sem("s_lnroot", ph)
            s_heads_f = sem("s_heads_f", ph)

            block = ph.enter_context(nc.Block())

            @block.sync
            def _(sp):
                sp.dma_start(dst_i[:, :], dst.rearrange("(p c) -> p c", p=EPR)).then_inc(s_edges, 16)
                sp.dma_start(src_i[:, :], src.rearrange("(p c) -> p c", p=EPR)).then_inc(s_edges, 16)
                sp.wait_ge(s_pad, 1)
                load_nodes(sp, h, s_x)
                sp.wait_ge(s_codes, 1)
                sp.dma_start(dst_d[0:E].rearrange("(p c) -> p c", p=EPR), dst16[:, :]).then_inc(s_stored, 16)
                sp.wait_ge(s_pads, 2)
                sp.dma_start(dst_d[E:EP].rearrange("(p c) -> p c", p=P), dstpad[:, :]).then_inc(s_stored, 16)
                sp.wait_ge(s_stored, 32)
                with nc.allow_non_contiguous_dma(reason="one element of each row, once"):
                    sp.dma_start(heads_i[:, :], dst_d[0:NSR * SR].rearrange("(a r c) -> a r c", a=1, c=SR)[:, :, 0]
                                 ).then_inc(s_heads, 16)
                sp.wait_ge(s_codes, 2)
                sp.dma_start(ql_d[0:E, :].rearrange("(p c) t -> p (c t)", p=EPR),
                             ql[:, :, :].rearrange("p c t -> p (c t)")).then_inc(s_stored, 16)
                for half in range(2):
                    sp.dma_start(ql_d[E:EP, :].rearrange("(q p c) t -> q p (c t)", q=2, p=P)[half],
                                 qlpad[:, :]).then_inc(s_stored, 16)
                sp.wait_ge(s_firstT, 1)
                sp.dma_start(first_d[0:NP].rearrange("(p c) -> p c", p=HI), firstT[:, :]).then_inc(s_first_d, 16)
                sp.dma_start(first_d[NP:NP + P].rearrange("(a c) -> a c", a=1), endc[:, :]).then_inc(s_first_d, 16)
                sp.dma_start(win_d[0:NW].rearrange("(p c) -> p c", p=HI), winT[:, :]).then_inc(s_first_d, 16)
                sp.dma_start(win_d[NW:NW + WN].rearrange("(a c) -> a c", a=1), endc[:, 0:WN]).then_inc(s_first_d, 16)
                sp.wait_ge(s_first_d, 64)
                sp.dma_start(nextT[:, :], first_d[1:NP + 1].rearrange("(p c) -> p c", p=HI)).then_inc(s_next, 16)
                sp.dma_start(winf[:, :], win_d.rearrange("(a c) -> a c", a=1).to_broadcast([P, NW + WN])
                             ).then_inc(s_next, 16)
                sp.wait_ge(s_disT, 1)
                sp.dma_start(dis_d.rearrange("(p c) -> p c", p=HI), rootT[:, :]).then_inc(s_stored, 16)
                sp.wait_ge(s_stored, 96)

            @block.gpsimd
            def _(pool):
                nc.gpsimd.iota(rel[:, :], [[1, P]], base=0, channel_multiplier=-1,
                               allow_small_or_imprecise_dtypes=True).then_inc(s_iota, 1)
                nc.gpsimd.iota(tgt[:, :], [[P, HI]], base=0, channel_multiplier=1,
                               allow_small_or_imprecise_dtypes=True).then_inc(s_iota, 1)
                nc.gpsimd.iota(iota_mv[:, :], [[1, MV]], base=0, channel_multiplier=0,
                               allow_small_or_imprecise_dtypes=True).then_inc(s_iota, 1)
                nc.gpsimd.iota(iota_lo[:, :, :], [[1, P], [0, WC]], base=0, channel_multiplier=0,
                               allow_small_or_imprecise_dtypes=True).then_inc(s_iota, 1)
                nc.gpsimd.memset(ones[:, :], 1.0).then_inc(s_iota, 1)
                nc.gpsimd.memset(dstpad[:, :], int(BIG)).then_inc(s_pads, 1)
                nc.gpsimd.memset(qlpad[:, :], -1.0).then_inc(s_pads, 1)
                nc.gpsimd.iota(cap[:, 0, :], [[WSLOTS, ROUNDS]], base=0, channel_multiplier=0,
                               allow_small_or_imprecise_dtypes=True).then_inc(s_iota, 1)
                nc.gpsimd.iota(cap[:, 1, :], [[ASLOTS, ROUNDS]], base=0, channel_multiplier=0,
                               allow_small_or_imprecise_dtypes=True).then_inc(s_iota, 1)
                nc.gpsimd.iota(wcode[:, :], [[MV, NW]], base=0, channel_multiplier=0,
                               allow_small_or_imprecise_dtypes=True).then_inc(s_iota, 1)
                nc.gpsimd.memset(endc[:, :], float(E)).then_inc(s_iota, 1)
                for k in range(HI):
                    if k % SB == 0:
                        pool.wait_ge(s_rows_i, k // SB + 1)
                    nc.gpsimd.indirect_dma_start(
                        out=rows[:, k, :], out_offset=None,
                        in_=dst_d[0:NSR * SR].rearrange("(r c) -> r c", c=SR),
                        in_offset=bass.IndirectOffsetOnAxis(ap=row_i[:, k:k + 1], axis=0)).then_inc(s_rows[k // SB], 16)

            @block.vector
            def _(dve):
                ch = Chain(dve, s_dve)
                nc.vector.memset(h[:, HI - 1, :], 0.0).then_inc(s_pad, 1)
                dve.wait_ge(s_iota, 1)
                nc.vector.tensor_scalar(ident[:, :], rel[:, :], 0.0, None, ALU.is_equal)
                ch.step(nc.vector.memset(inv[:, :], 1.0 / SC1))
                dve.wait_ge(s_edges, 32)
                nc.vector.tensor_copy(dst16[:, :], dst_i[:, :]).then_inc(s_codes, 1)
                ch.step(nc.vector.tensor_scalar(hi_i[:, :], src_i[:, :], 7, None, ALU.logical_shift_right))
                ch.link(nc.vector.tensor_scalar(src_i[:, :], src_i[:, :], P - 1, None, ALU.bitwise_and))
                ch.step(nc.vector.tensor_copy(ql[:, :, 1], src_i[:, :]))
                nc.vector.scalar_tensor_tensor(out=ql[:, :, 0], in0=dst_i[:, :], scalar=float(HI), in1=hi_i[:, :],
                                               op0=ALU.mult, op1=ALU.add).then_inc(s_codes, 1)

                def rows_below():
                    dve.wait_ge(s_heads, 16)
                    nc.vector.tensor_copy(heads[:, :], heads_i[:, :]).then_inc(s_heads_f, 1)
                    dve.wait_ge(s_heads_p, 1)
                    ch.link(nc.vector.tensor_copy(heads_b[:, :], heads_p[:, 0:NSR]))
                    dve.wait_ge(s_iota, 2)
                    for k in range(HI):
                        ch.reuse(k, 4)
                        ch.step(nc.vector.tensor_scalar(cmp[:, k % 4, 0:NSR], heads_b[:, :], tgt[:, k:k + 1], None,
                                                        ALU.is_lt, ALU.add, accum_out=cnt[:, k:k + 1]))
                        if k % SB == SB - 1:
                            ks = slice(k + 1 - SB, k + 1)
                            ch.wait()
                            ch.link(nc.vector.tensor_scalar(cnt[:, ks], cnt[:, ks], -1.0, 0.0, ALU.add, ALU.max))
                            nc.vector.tensor_copy(row_i[:, ks], cnt[:, ks]).then_inc(s_rows_i, 1)

                def act_root():
                    ch.link(nc.vector.tensor_copy(w[:, :], m[:, :]))
                    dve.sem_inc(s_lnvar, 1)
                    rows_below()
                    dve.wait_ge(s_lnroot, 1)

                dve.wait_ge(s_x, 32)
                layer_norm_relu(ch, act_root, h, t, m, r, w, y)
                for k in range(HI):
                    if k % SB == 0:
                        dve.wait_ge(s_rows[k // SB], 16 * SB)
                    ch.reuse(k, 4)
                    ch.step(nc.vector.tensor_scalar(cmp[:, k % 4, :], rows[:, k, :], tgt[:, k:k + 1], None,
                                                    ALU.is_lt, ALU.add, accum_out=cnt2[:, k:k + 1]))
                ch.wait()
                nc.vector.scalar_tensor_tensor(out=cnt[:, :], in0=cnt[:, :], scalar=float(SR), in1=cnt2[:, :],
                                               op0=ALU.mult, op1=ALU.add).then_inc(s_first, 1)
                dve.wait_ge(s_firstT_p, 1)
                ch.link(nc.vector.tensor_copy(firstT[:, :], firstT_p[:, :]))
                nc.vector.tensor_copy(winT[:, :], firstT[:, 0:P:WN]).then_inc(s_firstT, 1)
                dve.wait_ge(s_next, 32)
                ch.link(nc.vector.tensor_tensor(nextT[:, :], nextT[:, :], firstT[:, :], ALU.subtract))
                nc.vector.tensor_scalar(nextT[:, :], nextT[:, :], 1.0, 1.0, ALU.add, ALU.max).then_inc(s_var, 1)
                nc.vector.tensor_copy(win_i[:, :], winf[0:1, 0:NW])
                ch.step(nc.vector.tensor_tensor(len_w[:, :], winf[0:1, 1:NW + 1], winf[0:1, 0:NW], ALU.subtract))
                ch.link(nc.vector.tensor_tensor(len_g[:, :], winf[0:1, GW:NW + GW:GW], winf[0:1, 0:NW:GW],
                                                ALU.subtract))
                ch.step(nc.vector.tensor_reduce(mx[:, 0:1], len_w[:, :], AX.X, ALU.max))
                ch.link(nc.vector.tensor_reduce(mx[:, 1:2], len_g[:, :], AX.X, ALU.max))
                for k in range(2):
                    ch.link(nc.vector.tensor_scalar(cap[:, k, :], cap[:, k, :], mx[:, k:k + 1], None, ALU.is_lt,
                                                    ALU.add, accum_out=rnd[:, k:k + 1]))
                ch.link(nc.vector.tensor_copy(rounds_i[:, :], rnd[:, :]))
                dve.wait_ge(s_root, 1)
                inverse_root(ch, disT[:, :], rootT[:, :], nextT[:, :], tmpT[:, :])
                nc.vector.tensor_copy(rootT[:, :], disT[:, :]).then_inc(s_disT, 1)
                dve.wait_ge(s_dis_p, 1)
                ch.link(nc.vector.tensor_copy(dis[:, :], dis_p[:, :]))

            @block.scalar
            def _(act):
                act.wait_ge(s_lnvar, 1)
                nc.scalar.activation(r[:, :], m[:, :], ACT.Sqrt).then_inc(s_lnroot, 1)
                act.wait_ge(s_var, 1)
                nc.scalar.activation(rootT[:, :], nextT[:, :], ACT.Sqrt).then_inc(s_root, 1)

            @block.tensor
            def _(pe):
                pe.wait_ge(s_iota, 9)
                pe.wait_ge(s_heads_f, 1)
                nc.tensor.matmul(heads_p[:, 0:NSR], ones[:, :], heads[:, :], start=True, stop=True
                                 ).then_inc(s_heads_p, 1)
                pe.wait_ge(s_first, 1)
                nc.tensor.transpose(firstT_p[:, :], cnt[:, :], ident[:, :]).then_inc(s_firstT_p, 1)
                pe.wait_ge(s_disT, 1)
                nc.tensor.transpose(dis_p[:, :], rootT[:, :], ident[0:HI, 0:HI]).then_inc(s_dis_p, 1)

        with ExitStack() as ph:
            AU = 7
            rows = sb("arows", [P, AU, AC, EF], F32, ph)
            adst = sb("adst", [P, AU, AC], I16, ph)
            arel = sb("arel", [P, AU, 2, AC], F32, ph)
            hot = sb("ahot", [P, AU, AC, GN], F32, ph)
            agg = sb("agg", [EF, NP], F32, ph)
            pos = sb("pos", [P, AC], F32, ph)
            iota_n = sb("iota_n", [P, GN], F32, ph)
            gbase = sb("gbase", [P, NG], F32, ph)
            want = sb("want", [P, NG], F32, ph)
            over = sb("over", [P, NG], F32, ph)
            at_f = sb("at_f", [1, NG], F32, ph)
            at_i = sb("at_i", [1, NG], I32, ph)
            sdis = sb("sdis1", [P, HI], F32, ph)
            hT = sb("hT", [P, 2, TB * P], F32, ph)
            agg_p = [ps(f"agg_p{k}", [EF, GN], ph) for k in range(AU)]
            tp = ps("tp1", [P, TB * P], ph)

            s_const = sem("s_aconst", ph)
            s_off = sem("s_off", ph)
            s_loaded = [sem(f"s_loaded{k}", ph) for k in range(AU)]
            s_hot = sem("s_hot", ph)
            s_summed = sem("s_summed", ph)
            s_added = sem("s_added", ph)
            s_agg_d = sem("s_agg_d", ph)
            s_round = sem("s_round", ph)
            s_done = sem("s_adone", ph)
            s_dve = sem("s_adve", ph)
            s_sdis = sem("s_sdis1", ph)
            s_t = sem("s_t1", ph)
            s_hi = sem("s_hi1", ph)
            s_turned = sem("s_turned1", ph)
            s_kept = sem("s_kept1", ph)
            s_hT = [sem(f"s_hT{k}", ph) for k in range(2)]
            block = ph.enter_context(nc.Block())

            def attr_rounds(eng):
                return eng.value_load(rounds_i[0:1, 1:2], min_val=1, max_val=ROUNDS)

            @block.gpsimd
            def _(pool):
                nc.gpsimd.iota(pos[:, :], [[1, AC]], base=0, channel_multiplier=AC,
                               allow_small_or_imprecise_dtypes=True).then_inc(s_const, 1)
                nc.gpsimd.iota(iota_n[:, :], [[1, GN]], base=0, channel_multiplier=0,
                               allow_small_or_imprecise_dtypes=True).then_inc(s_const, 1)
                nc.gpsimd.iota(gbase[:, :], [[-GN, NG]], base=0, channel_multiplier=0,
                               allow_small_or_imprecise_dtypes=True).then_inc(s_const, 1)
                nc.gpsimd.memset(agg[:, :], 0.0).then_inc(s_const, 1)
                nc.gpsimd.tensor_scalar(sdis[:, :], dis[:, :], SC1, 0.0, ALU.mult, ALU.add).then_inc(s_sdis, 1)
                pool.wait_ge(s_sdis, 1)
                nc.gpsimd.tensor_tensor(t[:, :, :], h[:, :, :], sdis[:, :].unsqueeze(2).to_broadcast([P, HI, F]),
                                        ALU.mult).then_inc(s_t, 1)
                pool.wait_ge(s_hi, 1)
                nc.gpsimd.tensor_tensor(g_lo[:, :, :], t[:, :, :], g_hi[:, :, :], ALU.subtract)

            @block.scalar
            def _(act):
                for i, (k, n) in enumerate(BATCH):
                    act.wait_ge(s_turned, i + 1)
                    if i >= 2:
                        act.wait_ge(s_hT[i % 2], 16 * (i // 2))
                    nc.scalar.copy(hT[:, i % 2, 0:n * P], tp[:, 0:n * P]).then_inc(s_kept, 1)
                    act.wait_ge(s_kept, i + 1)
                    act.dma_start(hT_d[:, k * P:(k + n) * P], hT[:, i % 2, 0:n * P]).then_inc(s_hT[i % 2], 16)
                act.wait_ge(s_t, 1)
                nc.scalar.copy(g_hi[:, :, :], t[:, :, :]).then_inc(s_hi, 1)
                for q in range(2):
                    act.wait_ge(s_hT[q], 16 * len(BATCH[q::2]))

            @block.sync
            def _(sp):
                rounds = attr_rounds(sp)
                with sp.Fori(0, rounds) as r:
                    gate(sp, s_off, r + 1)
                    with sp.Fori(0, NG // AU) as i:
                        for k in range(AU):
                            at = sp.value_load(at_i[0:1, bass.ds(AU * i + k, 1)], min_val=0, max_val=E - ASLOTS)
                            sp.wait_ge(s_summed, (r * (NG // AU) + i) * AU + (k + 1))
                            sp.dma_start(rows[:, k, :, :].rearrange("p c f -> p (c f)"),
                                         attr[bass.ds(at, ASLOTS), :].rearrange("(p c) f -> p (c f)", p=P)
                                         ).then_inc(s_loaded[k], 16)
                            sp.dma_start(adst[:, k, :],
                                         dst_d[bass.ds(at, ASLOTS)].rearrange("(p c) -> p c", p=P)
                                         ).then_inc(s_loaded[k], 16)
                sp.wait_ge(s_done, rounds)
                sp.dma_start(agg_d, agg[:, :]).then_inc(s_agg_d, 16)
                sp.wait_ge(s_agg_d, 16)

            @block.tensor
            def _(pe):
                rounds = attr_rounds(pe)
                pe.sem_inc(s_summed, AU)
                for i, (k, n) in enumerate(BATCH):
                    if i >= 1:
                        pe.wait_ge(s_kept, i)
                    for c in range(n):
                        ins = nc.tensor.transpose(tp[:, c * P:(c + 1) * P], h[:, k + c, :], ident[:, :])
                    ins.then_inc(s_turned, 1)
                with pe.Fori(0, rounds) as r:
                    with pe.Fori(0, NG // AU) as i:
                        for k in range(AU):
                            pe.wait_ge(s_loaded[k], (r * (NG // AU) + i + 1) * 32)
                            pe.wait_ge(s_hot, (r * (NG // AU) + i) * AU + (k + 1))
                            pe.wait_ge(s_added, (r * (NG // AU) + i) * AU + (k + 1))
                            for c in range(AC):
                                ins = nc.tensor.matmul(agg_p[k][:, :], rows[:, k, c, :], hot[:, k, c, :],
                                                       start=(c == 0), stop=(c == AC - 1))
                            ins.then_inc(s_summed, 1)

            @block.vector
            def _(dve):
                ch = Chain(dve, s_dve)
                dve.sem_inc(s_added, AU)
                dve.wait_ge(s_const, 4)
                ch.link(nc.vector.tensor_copy(want[:, :], winf[:, 0:NW:GW]))
                rounds = attr_rounds(dve)

                def add_group(n, g, k):
                    dve.wait_ge(s_summed, n + (AU + 1))
                    nc.vector.tensor_tensor(agg[:, bass.ds(g * GN, GN)], agg[:, bass.ds(g * GN, GN)],
                                            agg_p[k][:, :], ALU.add).then_inc(s_added, 1)

                def hot_group(r, i, k):
                    n = (r * (NG // AU) + i) * AU + k
                    g = AU * i + k
                    dve.wait_ge(s_loaded[k], (r * (NG // AU) + i + 1) * 32)
                    dve.wait_ge(s_summed, n + 1)
                    nc.vector.tensor_scalar(arel[:, k, 0, :], pos[:, :], over[:, bass.ds(g, 1)], BIG,
                                            ALU.is_lt, ALU.mult).then_inc(s_dve, 1)
                    dve.wait_ge(s_dve, 2 * n + 2)
                    nc.vector.scalar_tensor_tensor(out=arel[:, k, 1, :], in0=adst[:, k, :],
                                                   scalar=gbase[:, bass.ds(g, 1)], in1=arel[:, k, 0, :],
                                                   op0=ALU.add, op1=ALU.add).then_inc(s_dve, 1)
                    dve.wait_ge(s_dve, 2 * n + 3)
                    nc.vector.tensor_tensor(hot[:, k, :, :], iota_n[:, :].unsqueeze(1).to_broadcast([P, AC, GN]),
                                            arel[:, k, 1, :].unsqueeze(2).to_broadcast([P, AC, GN]),
                                            ALU.is_equal).then_inc(s_hot, 1)

                LAG = 3
                with dve.Fori(0, rounds) as r:
                    nc.vector.tensor_scalar(at_f[:, :], want[0:1, :], float(E - ASLOTS), None, ALU.min
                                            ).then_inc(s_round, 1)
                    dve.wait_ge(s_round, r * 2 + 1)
                    nc.vector.tensor_copy(at_i[:, :], at_f[:, :]).then_inc(s_off, 1)
                    nc.vector.tensor_scalar(over[:, :], want[:, :], -float(E - ASLOTS), 0.0, ALU.add, ALU.max
                                            ).then_inc(s_round, 1)
                    gate(dve, s_round, r * 2 + 2)
                    n0 = r * NG
                    for k in range(AU):
                        hot_group(r, 0, k)
                        if k >= LAG:
                            add_group(n0 + (k - LAG), k - LAG, k - LAG)
                    with dve.Fori(1, NG // AU) as i:
                        for k in range(AU):
                            hot_group(r, i, k)
                            add_group(n0 + i * AU + (k - LAG), i * AU + (k - LAG), (k - LAG) % AU)
                    for k in range(AU - LAG, AU):
                        add_group(n0 + (NG - AU + k), NG - AU + k, k)
                    gate(dve, s_added, (r + 1) * NG + AU)
                    nc.vector.tensor_scalar(want[:, :], want[:, :], float(ASLOTS), None, ALU.add
                                            ).then_inc(s_done, 1)
                    gate(dve, s_done, r + 1)

        operand_ctx.close()

        def aggregate(layer, total):
            with ExitStack() as ph:
                RING = 4
                CW = 512
                NC = NP // CW
                slots = sb(f"slots{layer}", [P, RING, GW, WC, 2], F32, ph)
                code = sb(f"code{layer}", [P, RING, GW, WC], F32, ph)
                lo = sb(f"lo{layer}", [P, RING, GW, WC], F16, ph)
                mv = sb(f"mv{layer}", [P, GW, WC, MV], F16, ph)
                st = sb(f"st{layer}", [P, GW, P, WC], F16, ph)
                adj_all = sb(f"adj{layer}", [P, 2 * HI * CW], F16, ph)
                adj = adj_all[:, 0:2 * HI * BN].rearrange("p (b h n) -> p b h n", b=2, h=HI)
                adj_in = adj_all[:, :].rearrange("p (b h n) -> p b h n", b=2, h=HI)
                zeros = sb(f"zeros{layer}", [P, P], F16, ph)
                win_p = ps(f"win_p{layer}", [P, 4, 512], ph)
                dense_p = ps(f"dense_p{layer}", [P, 2, 512], ph)
                s_slots = [sem(f"s_slots{layer}_{h}", ph) for h in range(2)]
                slots_ready = sem(f"slots_ready{layer}", ph)
                codes_ready = sem(f"codes_ready{layer}", ph)
                hot_ready = sem(f"hot_ready{layer}", ph)
                built = sem(f"built{layer}", ph)
                evicted = sem(f"evicted{layer}", ph)
                saved = sem(f"saved{layer}", ph)
                dense_done = sem(f"dense_done{layer}", ph)
                taken = sem(f"taken{layer}", ph)
                zeroed = sem(f"zeroed{layer}", ph)
                in_ready = [sem(f"in_ready{layer}_{h}", ph) for h in range(2)]
                in_done = sem(f"in_done{layer}", ph)
                in_taken = sem(f"in_taken{layer}", ph)
                block = ph.enter_context(nc.Block())

                def load_rounds(eng):
                    return eng.value_load(rounds_i[0:1, 0:1], min_val=1, max_val=ROUNDS)

                def either(eng, rounds, build, load):
                    if layer == 1:
                        build(eng, rounds)
                    else:
                        with eng.If(rounds > 1):
                            build(eng, rounds)
                        with eng.Else():
                            load(eng)

                @block.sync
                def _(sp):
                    def build(sp, rounds):
                        sp.sem_inc(s_slots[1], 16)
                        with sp.Fori(0, rounds) as r:
                            with sp.Fori(0, NG // 2) as i:
                                for h in range(2):
                                    g = 2 * i + h
                                    _, at = nc.values_load_multi_w_load_instructions(
                                        win_i[0:1, bass.ds(g * GW, GW)], engines=(sp.engine,), min_val=0, max_val=E)
                                    sp.wait_ge(codes_ready, (r * NG + g) * 2 + 2)
                                    for k in range(GW):
                                        sp.dma_start(
                                            slots[:, bass.ds(g % RING, 1), k, :, :].rearrange("p a c t -> p (a c t)"),
                                            ql_d[bass.ds(at[k] + r * WSLOTS, WSLOTS), :]
                                            .rearrange("(p c) t -> p (c t)", p=P)).then_inc(s_slots[h], 16)
                                    gate(sp, s_slots[1 - h],
                                         (r * (NG // 2) + i) * (16 * GW) + (16 if h == 0 else 16 * GW))
                                    sp.sem_inc(slots_ready, 1)
                        gate(sp, s_slots[1], rounds * (NG // 2 * 16 * GW) + 16)
                        sp.sem_inc(slots_ready, 1)

                    def load(sp):
                        with sp.Fori(0, NC // 2) as c2:
                            for h in range(2):
                                sp.wait_ge(in_done, c2 * 2 + (h + 1))
                                sp.dma_start(adj_in[:, h, :, :], adj_d[:, :, bass.ds((c2 * 2 + h) * CW, CW)]
                                             ).then_inc(in_ready[h], 16)
                        sp.wait_ge(in_done, NC + 1)
                        sp.dma_start(adj_in[:, 0, :, 0:NP - NC * CW], adj_d[:, :, NC * CW:NP]
                                     ).then_inc(in_ready[0], 16)

                    either(sp, load_rounds(sp), build, load)

                @block.gpsimd
                def _(pool):
                    nc.gpsimd.memset(zeros[:, :], 0.0).then_inc(zeroed, 1)

                    def build(pool, rounds):
                        pool.sem_inc(codes_ready, 2 * RING)
                        with pool.Fori(0, rounds) as r:
                            with pool.Fori(0, NG) as g:
                                gate(pool, slots_ready, r * NG + g + 2)
                                gate(pool, hot_ready, (r * NG + g) * GW + GW)
                                nc.gpsimd.tensor_tensor(
                                    code[:, bass.ds(g % RING, 1), :, :].rearrange("p a w c -> p (a w) c"),
                                    slots[:, bass.ds(g % RING, 1), :, :, 0].rearrange("p a w c -> p (a w) c"),
                                    wcode[:, bass.ds(g * GW, GW)].unsqueeze(2).to_broadcast([P, GW, WC]),
                                    ALU.subtract).then_inc(codes_ready, 1)
                                nc.gpsimd.tensor_copy(
                                    lo[:, bass.ds(g % RING, 1), :, :].rearrange("p a w c -> p (a w) c"),
                                    slots[:, bass.ds(g % RING, 1), :, :, 1].rearrange("p a w c -> p (a w) c")
                                ).then_inc(codes_ready, 1)

                    either(pool, load_rounds(pool), build, lambda pool: pool.sem_inc(s_gate, 1))

                @block.vector
                def _(dve):
                    nc.vector.memset(total[:, :], 0.0).then_inc(zeroed, 1)
                    gate(dve, zeroed, 2)

                    def group(r, g):
                        n = r * NW + g * GW
                        gate(dve, codes_ready, (r * NG + g) * 2 + (2 * RING + 2))
                        for k in range(GW):
                            dve.wait_ge(built, n + (k + 1))
                            nc.vector.tensor_tensor(
                                st[:, k, :, :], iota_lo[:, :, :],
                                lo[:, bass.ds(g % RING, 1), k, :].to_broadcast([P, P, WC]), ALU.is_equal)
                            for c in range(WC):
                                ins = nc.vector.tensor_scalar(mv[:, k, c, :], iota_mv[:, :],
                                                              code[:, bass.ds(g % RING, 1), k, c], None, ALU.is_equal)
                            ins.then_inc(hot_ready, 1)

                    def add_block(r, b):
                        dve.wait_ge(dense_done, r * NB + b + 2)
                        nc.vector.tensor_tensor(
                            total[:, bass.ds(b * BN, BN)], total[:, bass.ds(b * BN, BN)],
                            dense_p[:, bass.ds(b % 2, 1), 0:BN].rearrange("p b n -> p (b n)"), ALU.add
                        ).then_inc(taken, 1)

                    def build(dve, rounds):
                        dve.sem_inc(taken, 2)
                        dve.sem_inc(hot_ready, RING * GW)
                        with dve.Fori(0, rounds) as r:
                            with dve.Fori(0, 2 * BG) as g:
                                group(r, g)
                            with dve.Fori(2, NB) as b:
                                group(r, b * BG)
                                add_block(r, b - 2)
                                with dve.Fori(1, BG) as j:
                                    group(r, b * BG + j)
                            add_block(r, NB - 2)
                            add_block(r, NB - 1)

                    either(dve, load_rounds(dve), build, lambda dve: dve.sem_inc(s_gate, 1))

                @block.scalar
                def _(act):
                    def build(act, rounds):
                        act.sem_inc(evicted, 4)
                        act.sem_inc(saved, 16)
                        with act.Fori(0, rounds) as r:
                            with act.Fori(0, NB) as b:
                                with act.Fori(0, BG) as j:
                                    for k in range(GW):
                                        gate(act, built, r * NW + b * (BG * GW) + j * GW + (GW + k + 1))
                                        nc.scalar.copy(
                                            adj[:, bass.ds(b % 2, 1), :, bass.ds(j * GN + k * WN, WN)]
                                            .rearrange("p b h d -> p d (b h)"),
                                            win_p[:, k % 4, 0:MV].rearrange("p (d h) -> p d h", d=WN)
                                        ).then_inc(evicted, 1)
                                if layer == 1:
                                    gate(act, saved, (r * NB + b) * 16 + 16)
                                    gate(act, evicted, r * NW + b * (BG * GW) + (BG * GW + 4))
                                    act.dma_start(adj_d[:, :, bass.ds(b * BN, BN)],
                                                  adj[:, bass.ds(b % 2, 1), :, :].rearrange("p b h n -> p (b h) n")
                                                  ).then_inc(saved, 16)
                        if layer == 1:
                            gate(act, saved, rounds * (NB * 16) + 16)

                    def load(act):
                        act.sem_inc(in_taken, 2)
                        with act.Fori(0, NC // 2) as c2:
                            for h in range(2):
                                gate(act, in_done, c2 * 2 + (h + 3))
                                nc.scalar.copy(total[:, bass.ds((c2 * 2 + h) * CW, CW)], dense_p[:, h, :]
                                               ).then_inc(in_taken, 1)
                        act.wait_ge(in_done, NC + 3)
                        nc.scalar.copy(total[:, NC * CW:NP], dense_p[:, 0, 0:NP - NC * CW])

                    either(act, load_rounds(act), build, load)

                @block.tensor
                def _(pe):
                    def build_window(r, i, k):
                        n = r * NW + i * GW + (k + 1)
                        pe.wait_ge(hot_ready, n + RING * GW)
                        pe.wait_ge(evicted, n)
                        for c in range(WC):
                            ins = nc.tensor.matmul(win_p[:, k % 4, 0:MV], st[:, k, :, c], mv[:, k, c, :],
                                                   start=(c == 0), stop=(c == WC - 1))
                        ins.then_inc(built, 1)

                    def bank(b):
                        return dense_p[:, bass.ds(b % 2, 1), 0:BN].rearrange("p b n -> p (b n)")

                    filler = g_hi[:, 0:BN // P + 1, :].rearrange("p h f -> p (h f)")[:, 0:BN]

                    def open_block(r, b):
                        gate(pe, evicted, r * NW + b * (BG * GW) + (BG * GW + 4))
                        gate(pe, taken, r * NB + b + 1)
                        nc.tensor.matmul(bank(b), zeros[:, :], filler, start=True, stop=False)

                    def multiply(b, j, k):
                        part = adj[:, bass.ds(b % 2, 1), bass.ds(j * HG + k, 1), :].rearrange("p b h n -> p (b h n)")
                        for g in (g_hi, g_lo):
                            nc.tensor.matmul(bank(b), g[:, bass.ds(j * HG + k, 1), :].rearrange("p h f -> p (h f)"),
                                             part, start=False, stop=False)

                    def close_block(b):
                        nc.tensor.matmul(bank(b), zeros[:, :], filler, start=False, stop=True
                                         ).then_inc(dense_done, 1)

                    def build(pe, rounds):
                        pe.sem_inc(built, GW)
                        pe.sem_inc(dense_done, 1)
                        gate(pe, zeroed, 2)
                        with pe.Fori(0, rounds) as r:
                            with pe.Fori(0, BG) as j:
                                for k in range(GW):
                                    build_window(r, j, k)
                            with pe.Fori(1, NB) as b:
                                open_block(r, b - 1)
                                with pe.Fori(0, BG) as j:
                                    for k in range(GW):
                                        build_window(r, b * BG + j, k)
                                        if k < HG:
                                            multiply(b - 1, j, k)
                                close_block(b - 1)
                            open_block(r, NB - 1)
                            with pe.Fori(0, BG) as j:
                                for k in range(HG):
                                    multiply(NB - 1, j, k)
                            close_block(NB - 1)

                    def load(pe):
                        pe.sem_inc(in_done, 2)
                        gate(pe, zeroed, 2)

                        def block_product(h, n):
                            for c in range(HI):
                                for g in (g_hi, g_lo):
                                    ins = nc.tensor.matmul(dense_p[:, h, 0:n], g[:, c, :], adj_in[:, h, c, 0:n],
                                                           start=(c == 0 and g is g_hi),
                                                           stop=(c == HI - 1 and g is g_lo))
                            ins.then_inc(in_done, 1)

                        with pe.Fori(0, NC // 2) as c2:
                            for h in range(2):
                                gate(pe, in_ready[h], (c2 + 1) * 16)
                                pe.wait_ge(in_taken, c2 * 2 + (h + 1))
                                block_product(h, CW)
                        pe.wait_ge(in_ready[0], (NC // 2 + 1) * 16)
                        pe.wait_ge(in_taken, NC + 1)
                        block_product(0, NP - NC * CW)

                    either(pe, load_rounds(pe), build, load)

        def after_aggregate(layer, total, W, b):
            with ExitStack() as ph:
                cur = sb(f"cur{layer}", [P, NP], F32, ph)
                disb = sb(f"disb{layer}", [P, NP], F32, ph)
                hn = sb(f"hn{layer}", [P, NP], F32, ph)
                W_sb = sb(f"W_sb{layer}", [P, F], F32, ph)
                b_sb = sb(f"b_sb{layer}", [P, 1], F32, ph)
                mx = sb(f"mx{layer}", [P, NB], F32, ph)
                m1 = sb(f"m1{layer}", [P, 1], F32, ph)
                sdis = sb(f"sdisl{layer}", [P, HI], F32, ph)
                node = sb(f"node{layer}", [P, HI, F], F32, ph)
                if layer == 2:
                    h0 = sb("h0", [P, NP], F32, ph)
                lin_p = ps(f"lin_p{layer}", [P, 2, 512], ph)
                tp = ps(f"tp_l{layer}", [P, 2, TB, P], ph)
                s_cur = sem(f"s_cur{layer}", ph)
                s_w = sem(f"s_w{layer}", ph)
                s_x = sem(f"s_x_l{layer}", ph)
                s_pad = sem(f"s_pad_l{layer}", ph)
                s_mixed = sem(f"s_mixed{layer}", ph)
                s_lin = sem(f"s_lin{layer}", ph)
                s_hn = sem(f"s_hn{layer}", ph)
                s_comb = sem(f"s_comb{layer}", ph)
                s_max = sem(f"s_max{layer}", ph)
                s_all = sem(f"s_all{layer}", ph)
                s_turned = sem(f"s_turned_l{layer}", ph)
                s_node = sem(f"s_node{layer}", ph)
                s_hi = sem(f"s_hi{layer}b", ph)
                s_out = sem(f"s_out{layer}", ph)
                s_dve = sem(f"s_dve_l{layer}", ph)
                block = ph.enter_context(nc.Block())

                @block.sync
                def _(sp):
                    sp.dma_start(disb[:, :], dis_d.rearrange("(a n) -> a n", a=1).to_broadcast([P, NP])
                                 ).then_inc(s_cur, 16)
                    sp.dma_start(cur[:, :], hT_d if layer == 1 else h1T_d).then_inc(s_cur, 16)
                    sp.dma_start(W_sb[:, :], W).then_inc(s_w, 16)
                    with nc.allow_non_contiguous_dma(reason="a bias, one element per partition"):
                        sp.dma_start(b_sb[:, :], b.rearrange("(p a) -> p a", a=1)).then_inc(s_w, 16)
                    if layer == 2:
                        sp.dma_start(h0[:, :], hT_d).then_inc(s_x, 16)
                        sp.wait_ge(s_pad, 1)
                        load_nodes(sp, node, s_x)
                        sp.wait_ge(s_node, len(BATCH))
                        sp.dma_start(x1_d, node[:, :, :].rearrange("p c f -> p (c f)")).then_inc(s_out, 16)
                    else:
                        sp.wait_ge(s_hn, NB)
                        sp.dma_start(h1T_d, hn[:, :]).then_inc(s_out, 16)
                    sp.wait_ge(s_out, 16)

                @block.gpsimd
                def _(pool):
                    if layer == 1:
                        pool.wait_ge(s_max, 1)
                        nc.gpsimd.partition_all_reduce(m1[:, :], m1[:, :], P, bass.bass_isa.ReduceOp.max
                                                       ).then_inc(s_all, 1)

                @block.vector
                def _(dve):
                    ch = Chain(dve, s_dve)
                    if layer == 2:
                        nc.vector.memset(node[:, HI - 1, :], 0.0).then_inc(s_pad, 1)
                    dve.wait_ge(s_cur, 32)
                    for c in range(NB):
                        cols = slice(c * BN, (c + 1) * BN)
                        ch.link(nc.vector.tensor_tensor(cur[:, cols], cur[:, cols], disb[:, cols], ALU.mult))
                        ch.link(nc.vector.scalar_tensor_tensor(out=total[:, cols], in0=total[:, cols],
                                                               scalar=inv[:, 0:1], in1=cur[:, cols],
                                                               op0=ALU.mult, op1=ALU.add))
                        nc.vector.tensor_tensor(total[:, cols], total[:, cols], disb[:, cols], ALU.mult
                                                ).then_inc(s_mixed, 1)
                    if layer == 1:
                        for c in range(NB):
                            dve.wait_ge(s_hn, c + 1)
                            ch.step(nc.vector.tensor_reduce(mx[:, c:c + 1], hn[:, c * BN:(c + 1) * BN], AX.X, ALU.max))
                        ch.wait()
                        nc.vector.tensor_reduce(m1[:, :], mx[:, :], AX.X, ALU.max).then_inc(s_max, 1)
                        dve.wait_ge(s_all, 1)
                        ch.link(nc.vector.tensor_scalar(m1[:, :], m1[:, :], 1.0 / TOP, 1e-30, ALU.mult, ALU.max))
                        ch.link(nc.vector.tensor_copy(inv[:, :], m1[:, :]))
                        ch.link(nc.vector.reciprocal(mx[:, 0:1], m1[:, :]))
                        ch.link(nc.vector.tensor_scalar(sdis[:, :], dis[:, :], mx[:, 0:1], None, ALU.mult))
                        for i, (k, n) in enumerate(BATCH):
                            dve.wait_ge(s_turned, i + 1)
                            nc.vector.tensor_tensor(node[:, k:k + n, :], tp[:, i % 2, 0:n, :],
                                                    sdis[:, k:k + n].unsqueeze(2).to_broadcast([P, n, F]),
                                                    ALU.mult).then_inc(s_node, 1)
                        for i, (k, n) in enumerate(BATCH):
                            dve.wait_ge(s_hi, i + 1)
                            nc.vector.tensor_tensor(g_lo[:, k:k + n, :], node[:, k:k + n, :], g_hi[:, k:k + n, :],
                                                    ALU.subtract)
                    else:
                        dve.wait_ge(s_x, 48)
                        for c in range(NB):
                            cols = slice(c * BN, (c + 1) * BN)
                            dve.wait_ge(s_hn, c + 1)
                            ch.link(nc.vector.tensor_tensor(hn[:, cols], hn[:, cols], h0[:, cols], ALU.add))
                            nc.vector.tensor_scalar(hn[:, cols], hn[:, cols], 0.5, None, ALU.mult).then_inc(s_comb, 1)
                        for i, (k, n) in enumerate(BATCH):
                            dve.wait_ge(s_turned, i + 1)
                            nc.vector.tensor_tensor(node[:, k:k + n, :], node[:, k:k + n, :], tp[:, i % 2, 0:n, :],
                                                    ALU.add).then_inc(s_node, 1)

                @block.scalar
                def _(act):
                    act.wait_ge(s_w, 32)
                    for c in range(NB):
                        act.wait_ge(s_lin, c + 1)
                        nc.scalar.activation(hn[:, c * BN:(c + 1) * BN], lin_p[:, c % 2, 0:BN], ACT.Relu,
                                             bias=b_sb[:, 0:1]).then_inc(s_hn, 1)
                    if layer == 1:
                        for i, (k, n) in enumerate(BATCH):
                            act.wait_ge(s_node, i + 1)
                            nc.scalar.copy(g_hi[:, k:k + n, :], node[:, k:k + n, :]).then_inc(s_hi, 1)

                @block.tensor
                def _(pe):
                    pe.wait_ge(s_w, 32)
                    for c in range(NB):
                        pe.wait_ge(s_mixed, c + 1)
                        if c >= 2:
                            pe.wait_ge(s_hn, c - 1)
                        nc.tensor.matmul(lin_p[:, c % 2, 0:BN], W_sb[:, :], total[:, c * BN:(c + 1) * BN],
                                         start=True, stop=True).then_inc(s_lin, 1)
                    pe.wait_ge(s_comb if layer == 2 else s_hn, NB)
                    for i, (k, n) in enumerate(BATCH):
                        if i >= 2:
                            pe.wait_ge(s_node, i - 1)
                        for c in range(n):
                            ins = nc.tensor.transpose(tp[:, i % 2, c, :], hn[:, (k + c) * P:(k + c + 1) * P],
                                                      ident[:, :])
                        ins.then_inc(s_turned, 1)

        def mlp():
            M1, M2 = w1.shape[1] // P, w2.shape[1] // P
            KU = F + EF
            SLOPE = 0.01
            CH = [(k, min(TB, HI - k)) for k in range(0, HI, TB)]
            with ExitStack() as ph:
                x1 = sb("x1", [P, HI, F], F32, ph)
                h = sb("hm", [P, HI, F], F32, ph)
                t = sb("tm", [P, HI, F], F32, ph)
                m, r, w, y = (sb(f"ln2_{n}", [P, HI], F32, ph) for n in "mrwy")
                agg = sb("agg_m", [EF, NP], F32, ph)
                w1a = sb("w1a", [P, M1 * P], F32, ph)
                w1b = sb("w1b", [EF, M1 * P], F32, ph)
                w1u = sb("w1u", [EF, M1 * P], F32, ph)
                w2_sb = sb("w2_sb", [P, M1, M2 * P], F32, ph)
                w3_sb = sb("w3_sb", [P, M2, F], F32, ph)
                u_sb = sb("u_sb", [EF, 1], F32, ph)
                c1_sb = sb("c1_sb", [P, M1], F32, ph)
                c2_sb = sb("c2_sb", [P, M2], F32, ph)
                c3_sb = sb("c3_sb", [1, F], F32, ph)
                hT = sb("hmT", [P, 2, TB * P], F32, ph)
                z1 = sb("z1", [P, 2, M1, TB * P], F32, ph)
                a1 = sb("a1", [P, 2, M1, TB * P], F32, ph)
                z2 = sb("z2", [P, 2, M2, TB * P], F32, ph)
                a2 = sb("a2", [P, 2, M2, TB * P], F32, ph)
                tp = ps("tpm", [P, TB * P], ph)
                z1_p = ps("z1_p", [P, M1, 512], ph)
                z2_p = ps("z2_p", [P, M2, 512], ph)
                y_p = ps("y_p", [P, 2, TB, F], ph)
                uc_p = ps("uc_p", [P, M1], ph)
                s_x = sem("s_xm", ph)
                s_w = sem("s_wm", ph)
                s_var = sem("s_varm", ph)
                s_root = sem("s_rootm", ph)
                s_h = sem("s_hm", ph)
                s_uc = sem("s_uc", ph)
                s_c1 = sem("s_c1", ph)
                s_turned = sem("s_turnedm", ph)
                s_hT = sem("s_hTm", ph)
                s_z1p = sem("s_z1p", ph)
                s_z1 = sem("s_z1", ph)
                s_a1 = sem("s_a1", ph)
                s_z2p = sem("s_z2p", ph)
                s_z2 = sem("s_z2", ph)
                s_a2 = sem("s_a2", ph)
                s_yp = sem("s_yp", ph)
                s_y = sem("s_y", ph)
                s_out = sem("s_outm", ph)
                s_dve = sem("s_dvem", ph)
                block = ph.enter_context(nc.Block())

                @block.sync
                def _(sp):
                    sp.dma_start(x1[:, :, :].rearrange("p c f -> p (c f)"), x1_d).then_inc(s_x, 16)
                    sp.dma_start(h[:, :, :].rearrange("p c f -> p (c f)"), x1_d).then_inc(s_x, 16)
                    sp.dma_start(agg[:, :], agg_d).then_inc(s_w, 16)
                    sp.dma_start(w1a[:, :], w1[0:F, :]).then_inc(s_w, 16)
                    sp.dma_start(w1b[:, :], w1[F:KU, :]).then_inc(s_w, 16)
                    sp.dma_start(w1u[:, :], w1[KU:KU + EF, :]).then_inc(s_w, 16)
                    sp.dma_start(w2_sb[:, :, :], w2.rearrange("(m p) n -> p m n", p=P)).then_inc(s_w, 16)
                    sp.dma_start(w3_sb[:, :, :], w3.rearrange("(m p) n -> p m n", p=P)).then_inc(s_w, 16)
                    sp.dma_start(c3_sb[:, :], c3.rearrange("(a n) -> a n", a=1)).then_inc(s_w, 16)
                    with nc.allow_non_contiguous_dma(reason="biases, one element per partition"):
                        sp.dma_start(u_sb[:, :], u[0:1, :].rearrange("a n -> n a")).then_inc(s_w, 16)
                        sp.dma_start(c1_sb[:, :], c1.rearrange("(m p) -> p m", p=P)).then_inc(s_w, 16)
                        sp.dma_start(c2_sb[:, :], c2.rearrange("(m p) -> p m", p=P)).then_inc(s_w, 16)
                    for i, (k, n) in enumerate(CH):
                        sp.wait_ge(s_y, i + 1)
                        full = n if k + n < HI else n - 1
                        if full:
                            sp.dma_start(out[k * P:(k + full) * P, :].rearrange("(c p) f -> p c f", p=P),
                                         x1[:, k:k + full, :]).then_inc(s_out, 16)
                        if full < n:
                            sp.dma_start(out[(HI - 1) * P:N, :], x1[0:TAIL, HI - 1, :]).then_inc(s_out, 16)
                    outs = len(CH) + (1 if CH[-1][1] > 1 else 0)
                    sp.wait_ge(s_out, 16 * outs)

                @block.vector
                def _(dve):
                    ch = Chain(dve, s_dve)
                    dve.wait_ge(s_x, 32)

                    def act_root():
                        ch.link(nc.vector.tensor_copy(w[:, :], m[:, :]))
                        dve.sem_inc(s_var, 1)
                        dve.wait_ge(s_root, 1)

                    layer_norm_relu(ch, act_root, h, t, m, r, w, y)
                    dve.sem_inc(s_h, 1)
                    dve.wait_ge(s_w, 160)
                    dve.wait_ge(s_uc, 1)
                    nc.vector.tensor_tensor(c1_sb[:, :], c1_sb[:, :], uc_p[:, :], ALU.add).then_inc(s_c1, 1)

                    def leaky(i, n, z, a, s_in, s_done):
                        dve.wait_ge(s_in, i + 1)
                        nc.vector.scalar_tensor_tensor(out=a[:, i % 2, :, 0:n * P], in0=z[:, i % 2, :, 0:n * P],
                                                       scalar=SLOPE, in1=z[:, i % 2, :, 0:n * P],
                                                       op0=ALU.mult, op1=ALU.max).then_inc(s_done, 1)

                    for i, (k, n) in enumerate(CH):
                        dve.wait_ge(s_turned, i + 1)
                        if i >= 2:
                            dve.wait_ge(s_z1p, i - 1)
                        nc.vector.tensor_copy(hT[:, i % 2, 0:n * P], tp[:, 0:n * P]).then_inc(s_hT, 1)
                        if i >= 2:
                            dve.wait_ge(s_z2p, i - 1)
                        leaky(i, n, z1, a1, s_z1, s_a1)
                        if i >= 2:
                            dve.wait_ge(s_yp, i - 1)
                        leaky(i, n, z2, a2, s_z2, s_a2)
                        dve.wait_ge(s_yp, i + 1)
                        nc.vector.tensor_tensor(x1[:, k:k + n, :], x1[:, k:k + n, :], y_p[:, i % 2, 0:n, :], ALU.add
                                                ).then_inc(s_y, 1)

                @block.scalar
                def _(act):
                    act.wait_ge(s_var, 1)
                    nc.scalar.activation(r[:, :], m[:, :], ACT.Sqrt).then_inc(s_root, 1)
                    act.wait_ge(s_c1, 1)
                    for i, (k, n) in enumerate(CH):
                        act.wait_ge(s_z1p, i + 1)
                        if i >= 2:
                            act.wait_ge(s_a1, i - 1)
                        for q in range(M1):
                            ins = nc.scalar.activation(z1[:, i % 2, q, 0:n * P], z1_p[:, q, 0:n * P], ACT.Identity,
                                                       bias=c1_sb[:, q:q + 1])
                        ins.then_inc(s_z1, 1)
                        act.wait_ge(s_z2p, i + 1)
                        if i >= 2:
                            act.wait_ge(s_a2, i - 1)
                        for q in range(M2):
                            ins = nc.scalar.activation(z2[:, i % 2, q, 0:n * P], z2_p[:, q, 0:n * P], ACT.Identity,
                                                       bias=c2_sb[:, q:q + 1])
                        ins.then_inc(s_z2, 1)

                @block.tensor
                def _(pe):
                    pe.wait_ge(s_w, 160)
                    for q in range(M1):
                        ins = nc.tensor.matmul(uc_p[:, q:q + 1], w1u[:, q * P:(q + 1) * P], u_sb[:, :],
                                               start=True, stop=True)
                    ins.then_inc(s_uc, 1)
                    pe.wait_ge(s_h, 1)
                    for i, (k, n) in enumerate(CH):
                        if i >= 1:
                            pe.wait_ge(s_hT, i)
                        for c in range(n):
                            ins = nc.tensor.transpose(tp[:, c * P:(c + 1) * P], h[:, k + c, :], ident[:, :])
                        ins.then_inc(s_turned, 1)
                        pe.wait_ge(s_hT, i + 1)
                        if i >= 1:
                            pe.wait_ge(s_z1, i)
                        for q in range(M1):
                            nc.tensor.matmul(z1_p[:, q, 0:n * P], w1a[:, q * P:(q + 1) * P], hT[:, i % 2, 0:n * P],
                                             start=True, stop=False)
                            ins = nc.tensor.matmul(z1_p[:, q, 0:n * P], w1b[:, q * P:(q + 1) * P],
                                                   agg[:, k * P:(k + n) * P], start=False, stop=True)
                        ins.then_inc(s_z1p, 1)
                        pe.wait_ge(s_a1, i + 1)
                        if i >= 1:
                            pe.wait_ge(s_z2, i)
                        for q in range(M2):
                            for c in range(M1):
                                ins = nc.tensor.matmul(z2_p[:, q, 0:n * P], w2_sb[:, c, q * P:(q + 1) * P],
                                                       a1[:, i % 2, c, 0:n * P], start=(c == 0), stop=(c == M1 - 1))
                        ins.then_inc(s_z2p, 1)
                        pe.wait_ge(s_a2, i + 1)
                        if i >= 2:
                            pe.wait_ge(s_y, i - 1)
                        for v in range(n):
                            nc.tensor.matmul(y_p[:, i % 2, v, :], ones[:, :], c3_sb[:, :], start=True, stop=False)
                            for c in range(M2):
                                ins = nc.tensor.matmul(y_p[:, i % 2, v, :], a2[:, i % 2, c, v * P:(v + 1) * P],
                                                       w3_sb[:, c, :], start=False, stop=(c == M2 - 1))
                        ins.then_inc(s_yp, 1)

        x1_d = scratch("x1_d", (P, HI * F), F32)
        with ExitStack() as ly:
            total = sb("total", [P, NP], F32, ly)
            aggregate(1, total)
            after_aggregate(1, total, W1, b1)
            aggregate(2, total)
            after_aggregate(2, total, W2, b2)
        mlp()


_INS = ['x', 'src', 'dst', 'edge_attr_64', 'L0_gnn_W1', 'L0_gnn_b1', 'L0_gnn_W2', 'L0_gnn_b2', 'L1_gnn_u',
        'L1_gnn_w1', 'L1_gnn_b1', 'L1_gnn_w2', 'L1_gnn_b2', 'L1_gnn_w3', 'L1_gnn_b3']


def kernel(**inputs):
    import numpy as _np
    import concourse.bacc as _bacc
    from concourse import mybir as _mybir
    from concourse.bass_utils import run_bass_kernel_spmd as _run

    nc = _bacc.Bacc("TRN2", target_bir_lowering=False, num_devices=1)
    arrays, args = {}, []
    for name in _INS:
        a = _np.ascontiguousarray(inputs[name])
        arrays[f"in_{name}_dram"] = a
        args.append(nc.dram_tensor(f"in_{name}_dram", a.shape, _mybir.dt.from_np(a.dtype), kind="ExternalInput").ap())
    out = nc.dram_tensor("out_0_dram", (6250, 128), _mybir.dt.float32, kind="ExternalOutput").ap()
    build(nc, *args, out)
    r = _run(nc, [arrays], core_ids=[0])
    return r.results[0]["out_0_dram"]
```

```python
from contextlib import ExitStack

import concourse.bass as bass
from concourse import mybir

ALU = mybir.AluOpType
ACT = mybir.ActivationFunctionType
AX = mybir.AxisListType
F32 = mybir.dt.float32
F16 = mybir.dt.float16
I32 = mybir.dt.int32
I16 = mybir.dt.int16

P = 128
N, F = 6250, 128
E = 206250
HI = -(-N // P)
NP = HI * P
TAIL = N - (HI - 1) * P

PN = 2
MV = PN * HI
WP = 4
WN = WP * PN
NW = NP // WN
GW = 8
UW = 4
UP = UW * WP
GU = GW // UW
GN = GW * WN
NG = NW // GW
BG = 7
NB = NG // BG
BN = BG * GN
HG = HI // BG
BP = BN // PN
TP = BP // 2
FETCHES = 2 * NB

AC = 19
ASLOTS = AC * P
EF = 64

EPR, EPC = 125, 1650
PADC = 2
EP = E + P * PADC
SB = 7
SR = 512
NSR = -(-E // SR)
BIG = 8192.0
FAR = 1e6
CLIP = 1000
SC1 = 4096.0
TOP = 16384.0
EPS = 1e-5
ROUNDS = -(-E // P) + 1


def build(nc, x, src, dst, attr, W1, b1, W2, b2, u, w1, c1, w2, c2, w3, c3, out):
    with ExitStack() as top:
        def sb(name, shape, dt, ctx=top):
            return ctx.enter_context(nc.sbuf_tensor(name, shape, dt))

        def ps(name, shape, ctx):
            return ctx.enter_context(nc.psum_tensor(name, shape, F32))

        def sem(name, ctx=top):
            return ctx.enter_context(nc.semaphore(name))

        def scratch(name, shape, dt):
            return nc.dram_tensor(name, shape, dt, kind="Internal").ap()

        ql_d = scratch("ql_d", (EP, 2), F32)
        dst_d = scratch("dst_d", (EP,), I16)
        first_d = scratch("first_d", (NP + P,), F32)
        group_d = scratch("group_d", (NG + 2,), F32)
        dis_d = scratch("dis_d", (NP,), F32)
        hT_d = scratch("hT_d", (F, NP), F32)
        h1T_d = scratch("h1T_d", (F, NP), F32)
        adj_d = scratch("adj_d", (P, HI, NP), F16)
        agg_d = scratch("agg_d", (EF, NP), F32)

        ident = sb("ident", [P, P], F32)
        ones = sb("ones", [1, P], F32)
        dis = sb("dis", [P, HI], F32)
        gstart = sb("gstart", [P, NG + 2], F32)
        pstart = sb("pstart", [TP, FETCHES], F32)
        pcode = sb("pcode", [TP, FETCHES], F32)
        rounds_i = sb("rounds_i", [1, 2], I32)
        iota_mv = sb("iota_mv", [P, MV], F16)
        iota_lo = sb("iota_lo", [P, P], F16)
        g_hi = sb("g_hi", [P, HI, F], F16)
        g_lo = sb("g_lo", [P, HI, F], F16)
        inv = sb("inv", [P, 1], F32)
        scale2 = sb("scale2", [P, 1], F32)
        inv2 = sb("inv2", [P, 1], F32)
        W1_sb = sb("W1_sb", [P, F], F32)
        b1_sb = sb("b1_sb", [P, 1], F32)

        class Chain:

            def __init__(self, eng, s):
                self.eng, self.s, self.n = eng, s, 0

            def step(self, ins):
                self.n += 1
                ins.then_inc(self.s, 1)

            def wait(self):
                self.eng.wait_ge(self.s, self.n)

            def link(self, ins):
                self.step(ins)
                self.wait()

            def reuse(self, k, depth):
                if k >= depth:
                    self.eng.wait_ge(self.s, self.n - depth + 1)

        s_gate = sem("s_gate")

        def gate(eng, s, value):
            eng.wait_ge(s, value)
            eng.sem_inc(s_gate, 1)

        def inverse_root(ch, y, root, d, t):
            ch.link(nc.vector.reciprocal(y, root))
            ch.link(nc.vector.tensor_tensor(t, y, y, ALU.mult))
            ch.link(nc.vector.tensor_tensor(t, t, d, ALU.mult))
            ch.link(nc.vector.tensor_scalar(t, t, -0.5, 1.5, ALU.mult, ALU.add))
            ch.link(nc.vector.tensor_tensor(y, y, t, ALU.mult))

        TB = 4
        NT = 4
        CW = NT * P
        BATCH = [(k, min(TB, HI - k)) for k in range(0, HI, TB)]

        def load_nodes(sp, tile, s):
            sp.dma_start(tile[:, 0:HI - 1, :], x[0:(HI - 1) * P, :].rearrange("(c p) f -> p c f", p=P)).then_inc(s, 16)
            sp.dma_start(tile[0:TAIL, HI - 1, :], x[(HI - 1) * P:N, :]).then_inc(s, 16)

        operand_ctx = top.enter_context(ExitStack())
        h = sb("h", [P, HI, F], F32, operand_ctx)
        t = sb("h_t", [P, HI, F], F32, operand_ctx)

        with ExitStack() as ph:
            src_i = sb("src_i", [EPR, EPC], I32, ph)
            dst_i = sb("dst_i", [EPR, EPC], I32, ph)
            hi_i = sb("hi_i", [EPR, EPC], I32, ph)
            ql = sb("ql", [EPR, EPC, 2], F32, ph)
            dst16 = sb("dst16", [EPR, EPC], I16, ph)
            qlpad = sb("qlpad", [P, PADC * 2], F32, ph)
            dstpad = sb("dstpad", [P, PADC], I16, ph)
            rel = sb("rel", [P, P], F32, ph)
            tgt = sb("tgt", [P, HI], F32, ph)
            heads_i = sb("heads_i", [1, NSR], I16, ph)
            heads = sb("heads", [1, NSR], F32, ph)
            heads_b = sb("heads_b", [P, NSR], I16, ph)
            rows = sb("rows", [P, HI, SR], I16, ph)
            cmp = sb("cmp", [P, 4, SR], F16, ph)
            cnt = sb("cnt", [P, HI], F32, ph)
            cnt2 = sb("cnt2", [P, HI], F32, ph)
            row_i = sb("row_i", [P, HI], I32, ph)
            firstT = sb("firstT", [HI, P], F32, ph)
            nextT = sb("nextT", [HI, P], F32, ph)
            disT = sb("disT", [HI, P], F32, ph)
            rootT = sb("rootT", [HI, P], F32, ph)
            tmpT = sb("tmpT", [HI, P], F32, ph)
            groupT = sb("groupT", [HI, P // GN], F32, ph)
            pairT = sb("pairT", [HI, P // PN], F32, ph)
            mxT = sb("mxT", [HI, 1], F32, ph)
            endc = sb("endc", [1, P], F32, ph)
            cap = sb("cap", [1, 2, ROUNDS], F32, ph)
            len_g = sb("len_g", [1, NG], F32, ph)
            mx = sb("mx", [1, 2], F32, ph)
            rnd = sb("rnd", [1, 2], F32, ph)
            stats = sb("stats1", [P, HI, 6], F32, ph)
            mean_var = sb("mean_var1", [P, HI, 2], F32, ph)
            var, root, tmp, rstd, shift = (sb(f"{n}_x", [P, HI], F32, ph)
                                           for n in ("var", "root", "tmp", "rstd", "shift"))
            heads_p = ps("heads_p", [P, 512], ph)
            firstT_p = ps("firstT_p", [HI, P], ph)
            dis_p = ps("dis_p", [P, HI], ph)
            mx_p = ps("mx_p", [1, HI], ph)
            tp = ps("tp1", [P, TB * P], ph)
            hT = sb("hT", [P, 2, TB * P], F32, ph)
            s_h = sem("s_h1", ph)
            s_turned = sem("s_turned1", ph)
            s_kept = sem("s_kept1", ph)
            s_hT = [sem(f"s_hT{k}", ph) for k in range(2)]

            s_edges = sem("s_edges", ph)
            s_iota = sem("s_iota", ph)
            s_codes = sem("s_codes", ph)
            s_pads = sem("s_pads", ph)
            s_stored = sem("s_stored", ph)
            s_heads = sem("s_heads", ph)
            s_heads_p = sem("s_heads_p", ph)
            s_rows_i = sem("s_rows_i", ph)
            s_rows = [sem(f"s_rows{b}", ph) for b in range(HI // SB)]
            s_first = sem("s_first", ph)
            s_firstT_p = sem("s_firstT_p", ph)
            s_firstT = sem("s_firstT", ph)
            s_first_d = sem("s_first_d", ph)
            s_next = sem("s_next", ph)
            s_root = sem("s_root", ph)
            s_var = sem("s_var", ph)
            s_mxT = sem("s_mxT", ph)
            s_mx_p = sem("s_mx_p", ph)
            s_disT = sem("s_disT", ph)
            s_dis_p = sem("s_dis_p", ph)
            s_dve = sem("s_dve", ph)
            s_pad = sem("s_pad1", ph)
            s_x = sem("s_x1", ph)
            s_lnvar = sem("s_lnvar", ph)
            s_lnroot = sem("s_lnroot", ph)
            s_shift = sem("s_shift", ph)
            s_w = sem("s_w1", ph)
            s_heads_f = sem("s_heads_f", ph)

            block = ph.enter_context(nc.Block())

            @block.sync
            def _(sp):
                sp.dma_start(dst_i[:, :], dst.rearrange("(p c) -> p c", p=EPR)).then_inc(s_edges, 16)
                sp.dma_start(src_i[:, :], src.rearrange("(p c) -> p c", p=EPR)).then_inc(s_edges, 16)
                sp.wait_ge(s_pad, 1)
                load_nodes(sp, h, s_x)
                sp.dma_start(W1_sb[:, :], W1).then_inc(s_w, 16)
                with nc.allow_non_contiguous_dma(reason="a bias, one element per partition"):
                    sp.dma_start(b1_sb[:, :], b1.rearrange("(p a) -> p a", a=1)).then_inc(s_w, 16)
                sp.wait_ge(s_codes, 1)
                sp.dma_start(dst_d[0:E].rearrange("(p c) -> p c", p=EPR), dst16[:, :]).then_inc(s_stored, 16)
                sp.wait_ge(s_pads, 3)
                sp.dma_start(dst_d[E:EP].rearrange("(p c) -> p c", p=P), dstpad[:, :]).then_inc(s_stored, 16)
                sp.wait_ge(s_stored, 32)
                with nc.allow_non_contiguous_dma(reason="one element of each row, once"):
                    sp.dma_start(heads_i[:, :], dst_d[0:NSR * SR].rearrange("(a r c) -> a r c", a=1, c=SR)[:, :, 0]
                                 ).then_inc(s_heads, 16)
                sp.wait_ge(s_codes, 2)
                sp.dma_start(ql_d[0:E, :].rearrange("(p c) t -> p (c t)", p=EPR),
                             ql[:, :, :].rearrange("p c t -> p (c t)")).then_inc(s_stored, 16)
                sp.dma_start(ql_d[E:EP, :].rearrange("(p c) t -> p (c t)", p=P), qlpad[:, :]).then_inc(s_stored, 16)
                sp.wait_ge(s_firstT, 1)
                sp.dma_start(first_d[0:NP].rearrange("(p c) -> p c", p=HI), firstT[:, :]).then_inc(s_first_d, 16)
                sp.dma_start(first_d[NP:NP + P].rearrange("(a c) -> a c", a=1), endc[:, :]).then_inc(s_first_d, 16)
                sp.dma_start(group_d[0:NG].rearrange("(p c) -> p c", p=HI), groupT[:, :]).then_inc(s_first_d, 16)
                sp.dma_start(group_d[NG:NG + 2].rearrange("(a c) -> a c", a=1), endc[:, 0:2]).then_inc(s_first_d, 16)
                sp.wait_ge(s_first_d, 64)
                sp.dma_start(nextT[:, :], first_d[1:NP + 1].rearrange("(p c) -> p c", p=HI)).then_inc(s_next, 16)
                sp.dma_start(gstart[:, :], group_d.rearrange("(a c) -> a c", a=1).to_broadcast([P, NG + 2])
                             ).then_inc(s_next, 16)
                with nc.allow_non_contiguous_dma(reason="every other node's first edge, once"):
                    sp.dma_start(pstart[:, :], first_d[0:NP].rearrange("(b p t) -> p b t", p=TP, t=PN)[:, :, 0]
                                 ).then_inc(s_next, 16)
                sp.wait_ge(s_disT, 1)
                sp.dma_start(dis_d.rearrange("(p c) -> p c", p=HI), rootT[:, :]).then_inc(s_stored, 16)
                sp.wait_ge(s_next, 48)
                sp.wait_ge(s_w, 32)
                sp.wait_ge(s_stored, 80)

            @block.gpsimd
            def _(pool):
                nc.gpsimd.iota(rel[:, :], [[1, P]], base=0, channel_multiplier=-1,
                               allow_small_or_imprecise_dtypes=True).then_inc(s_iota, 1)
                nc.gpsimd.iota(tgt[:, :], [[P, HI]], base=0, channel_multiplier=1,
                               allow_small_or_imprecise_dtypes=True).then_inc(s_iota, 1)
                nc.gpsimd.iota(iota_mv[:, :], [[1, MV]], base=0, channel_multiplier=0,
                               allow_small_or_imprecise_dtypes=True).then_inc(s_iota, 1)
                nc.gpsimd.iota(iota_lo[:, :], [[1, P]], base=0, channel_multiplier=0,
                               allow_small_or_imprecise_dtypes=True).then_inc(s_iota, 1)
                nc.gpsimd.memset(ones[:, :], 1.0).then_inc(s_iota, 1)
                nc.gpsimd.memset(dstpad[:, :], int(BIG)).then_inc(s_pads, 1)
                nc.gpsimd.memset(qlpad[:, 0:PADC * 2:2], FAR).then_inc(s_pads, 1)
                nc.gpsimd.memset(qlpad[:, 1:PADC * 2:2], 0.0).then_inc(s_pads, 1)
                nc.gpsimd.iota(cap[:, 0, :], [[P, ROUNDS]], base=0, channel_multiplier=0,
                               allow_small_or_imprecise_dtypes=True).then_inc(s_iota, 1)
                nc.gpsimd.iota(cap[:, 1, :], [[ASLOTS, ROUNDS]], base=0, channel_multiplier=0,
                               allow_small_or_imprecise_dtypes=True).then_inc(s_iota, 1)
                nc.gpsimd.iota(pcode[:, :], [[MV * TP, FETCHES]], base=0, channel_multiplier=MV,
                               allow_small_or_imprecise_dtypes=True).then_inc(s_iota, 1)
                nc.gpsimd.memset(endc[:, :], float(E)).then_inc(s_iota, 1)
                for k in range(HI):
                    if k % SB == 0:
                        pool.wait_ge(s_rows_i, k // SB + 1)
                    nc.gpsimd.indirect_dma_start(
                        out=rows[:, k, :], out_offset=None,
                        in_=dst_d[0:NSR * SR].rearrange("(r c) -> r c", c=SR),
                        in_offset=bass.IndirectOffsetOnAxis(ap=row_i[:, k:k + 1], axis=0)).then_inc(s_rows[k // SB], 16)

            @block.vector
            def _(dve):
                ch = Chain(dve, s_dve)
                nc.vector.memset(h[:, HI - 1, :], 0.0).then_inc(s_pad, 1)
                dve.wait_ge(s_iota, 1)
                nc.vector.tensor_scalar(ident[:, :], rel[:, :], 0.0, None, ALU.is_equal)
                ch.step(nc.vector.memset(inv[:, :], 1.0 / SC1))
                dve.wait_ge(s_edges, 32)
                nc.vector.tensor_copy(dst16[:, :], dst_i[:, :]).then_inc(s_codes, 1)
                ch.step(nc.vector.tensor_scalar(hi_i[:, :], src_i[:, :], 7, None, ALU.logical_shift_right))
                ch.link(nc.vector.tensor_scalar(src_i[:, :], src_i[:, :], P - 1, None, ALU.bitwise_and))
                ch.step(nc.vector.tensor_copy(ql[:, :, 1], src_i[:, :]))
                nc.vector.scalar_tensor_tensor(out=ql[:, :, 0], in0=dst_i[:, :], scalar=float(HI), in1=hi_i[:, :],
                                               op0=ALU.mult, op1=ALU.add).then_inc(s_codes, 1)

                dve.wait_ge(s_heads, 16)
                nc.vector.tensor_copy(heads[:, :], heads_i[:, :]).then_inc(s_heads_f, 1)
                dve.wait_ge(s_heads_p, 1)
                ch.link(nc.vector.tensor_copy(heads_b[:, :], heads_p[:, 0:NSR]))
                dve.wait_ge(s_iota, 2)
                for k in range(HI):
                    ch.reuse(k, 4)
                    ch.step(nc.vector.tensor_scalar(cmp[:, k % 4, 0:NSR], heads_b[:, :], tgt[:, k:k + 1], None,
                                                    ALU.is_lt, ALU.add, accum_out=cnt[:, k:k + 1]))
                    if k % SB == SB - 1:
                        ks = slice(k + 1 - SB, k + 1)
                        ch.wait()
                        ch.link(nc.vector.tensor_scalar(cnt[:, ks], cnt[:, ks], -1.0, 0.0, ALU.add, ALU.max))
                        nc.vector.tensor_copy(row_i[:, ks], cnt[:, ks]).then_inc(s_rows_i, 1)
                dve.wait_ge(s_x, 32)
                for k in range(HI):
                    ch.step(nc.vector.bn_stats(stats[:, k, :], h[:, k, :]))
                ch.wait()
                for k in range(HI):
                    ch.step(nc.vector.bn_aggr(mean_var[:, k, :], stats[:, k, :]))
                ch.wait()
                nc.vector.tensor_scalar(var[:, :], mean_var[:, :, 1], EPS, None, ALU.add).then_inc(s_lnvar, 1)
                dve.wait_ge(s_lnroot, 1)
                inverse_root(ch, rstd[:, :], root[:, :], var[:, :], tmp[:, :])
                nc.vector.scalar_tensor_tensor(out=shift[:, :], in0=mean_var[:, :, 0], scalar=-1.0, in1=rstd[:, :],
                                               op0=ALU.mult, op1=ALU.mult).then_inc(s_shift, 1)
                for k in range(HI):
                    if k % SB == 0:
                        dve.wait_ge(s_rows[k // SB], 16 * SB)
                    ch.reuse(k, 4)
                    ch.step(nc.vector.tensor_scalar(cmp[:, k % 4, :], rows[:, k, :], tgt[:, k:k + 1], None,
                                                    ALU.is_lt, ALU.add, accum_out=cnt2[:, k:k + 1]))
                ch.wait()
                nc.vector.scalar_tensor_tensor(out=cnt[:, :], in0=cnt[:, :], scalar=float(SR), in1=cnt2[:, :],
                                               op0=ALU.mult, op1=ALU.add).then_inc(s_first, 1)
                dve.wait_ge(s_firstT_p, 1)
                ch.link(nc.vector.tensor_copy(firstT[:, :], firstT_p[:, :]))
                nc.vector.tensor_copy(groupT[:, :], firstT[:, 0:P:GN]).then_inc(s_firstT, 1)
                dve.wait_ge(s_next, 48)
                ch.link(nc.vector.tensor_tensor(pairT[:, :], nextT[:, PN - 1:P:PN], firstT[:, 0:P:PN], ALU.subtract))
                nc.vector.tensor_reduce(mxT[:, :], pairT[:, :], AX.X, ALU.max).then_inc(s_mxT, 1)
                ch.link(nc.vector.tensor_tensor(nextT[:, :], nextT[:, :], firstT[:, :], ALU.subtract))
                nc.vector.tensor_scalar(nextT[:, :], nextT[:, :], 1.0, 1.0, ALU.add, ALU.max).then_inc(s_var, 1)
                ch.link(nc.vector.tensor_tensor(len_g[:, :], gstart[0:1, 1:NG + 1], gstart[0:1, 0:NG], ALU.subtract))
                ch.step(nc.vector.tensor_reduce(mx[:, 1:2], len_g[:, :], AX.X, ALU.max))
                dve.wait_ge(s_mx_p, 1)
                ch.link(nc.vector.tensor_reduce(mx[:, 0:1], mx_p[:, :], AX.X, ALU.max))
                for k in range(2):
                    ch.link(nc.vector.tensor_scalar(cap[:, k, :], cap[:, k, :], mx[:, k:k + 1], None, ALU.is_lt,
                                                    ALU.add, accum_out=rnd[:, k:k + 1]))
                ch.link(nc.vector.tensor_copy(rounds_i[:, :], rnd[:, :]))
                dve.wait_ge(s_root, 1)
                inverse_root(ch, disT[:, :], rootT[:, :], nextT[:, :], tmpT[:, :])
                nc.vector.tensor_copy(rootT[:, :], disT[:, :]).then_inc(s_disT, 1)
                dve.wait_ge(s_dis_p, 1)
                ch.link(nc.vector.tensor_copy(dis[:, :], dis_p[:, :]))

            @block.scalar
            def _(act):
                act.wait_ge(s_lnvar, 1)
                nc.scalar.activation(root[:, :], var[:, :], ACT.Sqrt).then_inc(s_lnroot, 1)
                act.wait_ge(s_shift, 1)

                def keep(i):
                    k, n = BATCH[i]
                    act.wait_ge(s_turned, i + 1)
                    if i >= 2:
                        act.wait_ge(s_hT[i % 2], 16 * (i // 2))
                    nc.scalar.copy(hT[:, i % 2, 0:n * P], tp[:, 0:n * P]).then_inc(s_kept, 1)
                    act.wait_ge(s_kept, i + 1)
                    act.dma_start(hT_d[:, k * P:(k + n) * P], hT[:, i % 2, 0:n * P]).then_inc(s_hT[i % 2], 16)

                for i, (k, n) in enumerate(BATCH):
                    for c in range(k, k + n):
                        ins = nc.scalar.activation(h[:, c, :], h[:, c, :], ACT.Relu, bias=shift[:, c:c + 1],
                                                   scale=rstd[:, c:c + 1])
                    ins.then_inc(s_h, 1)
                    if i >= 1:
                        keep(i - 1)
                keep(len(BATCH) - 1)
                act.wait_ge(s_var, 1)
                nc.scalar.activation(rootT[:, :], nextT[:, :], ACT.Sqrt).then_inc(s_root, 1)
                for q in range(2):
                    act.wait_ge(s_hT[q], 16 * len(BATCH[q::2]))

            @block.tensor
            def _(pe):
                pe.wait_ge(s_iota, 9)
                pe.wait_ge(s_heads_f, 1)
                nc.tensor.matmul(heads_p[:, 0:NSR], ones[:, :], heads[:, :], start=True, stop=True
                                 ).then_inc(s_heads_p, 1)
                for i, (k, n) in enumerate(BATCH):
                    if i == len(BATCH) - 3:
                        pe.wait_ge(s_first, 1)
                        nc.tensor.transpose(firstT_p[:, :], cnt[:, :], ident[:, :]).then_inc(s_firstT_p, 1)
                    pe.wait_ge(s_h, i + 1)
                    if i >= 1:
                        pe.wait_ge(s_kept, i)
                    for c in range(n):
                        ins = nc.tensor.transpose(tp[:, c * P:(c + 1) * P], h[:, k + c, :], ident[:, :])
                    ins.then_inc(s_turned, 1)
                pe.wait_ge(s_mxT, 1)
                nc.tensor.transpose(mx_p[:, :], mxT[:, :], ident[0:HI, 0:HI]).then_inc(s_mx_p, 1)
                pe.wait_ge(s_disT, 1)
                nc.tensor.transpose(dis_p[:, :], rootT[:, :], ident[0:HI, 0:HI]).then_inc(s_dis_p, 1)

        with ExitStack() as ph:
            AU = 7
            rows = sb("arows", [P, AU, AC, EF], F32, ph)
            adst = sb("adst", [P, AU, AC], I16, ph)
            arel = sb("arel", [P, AU, 2, AC], F32, ph)
            hot = sb("ahot", [P, AU, AC, GN], F32, ph)
            agg = sb("agg", [EF, NP], F32, ph)
            pos = sb("pos", [P, AC], F32, ph)
            iota_n = sb("iota_n", [P, GN], F32, ph)
            gbase = sb("gbase", [P, NG], F32, ph)
            want = sb("want", [P, NG], F32, ph)
            over = sb("over", [P, NG], F32, ph)
            at_f = sb("at_f", [1, NG], F32, ph)
            at_i = sb("at_i", [1, NG], I32, ph)
            sdis = sb("sdis1", [P, HI], F32, ph)
            agg_p = [ps(f"agg_p{k}", [EF, GN], ph) for k in range(AU)]
            norm_p = ps("norm_p", [P, 1], ph)
            square = sb("square", [P, F], F32, ph)
            ones_p = sb("ones_p", [P, 1], F32, ph)
            norm = sb("norm", [P, 1], F32, ph)
            bound = sb("bound", [P, 1], F32, ph)

            s_square = sem("s_square", ph)
            s_norm_p = sem("s_norm_p", ph)
            s_norm = sem("s_norm", ph)
            s_bound = sem("s_bound", ph)
            s_const = sem("s_aconst", ph)
            s_off = sem("s_off", ph)
            s_loaded = [sem(f"s_loaded{k}", ph) for k in range(AU)]
            s_hot = sem("s_hot", ph)
            s_summed = sem("s_summed", ph)
            s_added = sem("s_added", ph)
            s_agg_d = sem("s_agg_d", ph)
            s_round = sem("s_round", ph)
            s_done = sem("s_adone", ph)
            s_dve = sem("s_adve", ph)
            s_sdis = sem("s_sdis1", ph)
            s_t = sem("s_t1", ph)
            s_hi = sem("s_hi1", ph)
            block = ph.enter_context(nc.Block())

            def attr_rounds(eng):
                return eng.value_load(rounds_i[0:1, 1:2], min_val=1, max_val=ROUNDS)

            @block.gpsimd
            def _(pool):
                nc.gpsimd.iota(pos[:, :], [[1, AC]], base=0, channel_multiplier=AC,
                               allow_small_or_imprecise_dtypes=True).then_inc(s_const, 1)
                nc.gpsimd.iota(iota_n[:, :], [[1, GN]], base=0, channel_multiplier=0,
                               allow_small_or_imprecise_dtypes=True).then_inc(s_const, 1)
                nc.gpsimd.iota(gbase[:, :], [[-GN, NG]], base=0, channel_multiplier=0,
                               allow_small_or_imprecise_dtypes=True).then_inc(s_const, 1)
                nc.gpsimd.memset(agg[:, :], 0.0).then_inc(s_const, 1)
                nc.gpsimd.tensor_scalar(sdis[:, :], dis[:, :], SC1, 0.0, ALU.mult, ALU.add).then_inc(s_sdis, 1)
                pool.wait_ge(s_sdis, 1)
                nc.gpsimd.tensor_tensor(t[:, :, :], h[:, :, :], sdis[:, :].unsqueeze(2).to_broadcast([P, HI, F]),
                                        ALU.mult).then_inc(s_t, 1)
                pool.wait_ge(s_hi, 1)
                nc.gpsimd.tensor_tensor(g_lo[:, :, :], t[:, :, :], g_hi[:, :, :], ALU.subtract)
                pool.wait_ge(s_bound, 3)
                nc.gpsimd.partition_all_reduce(bound[:, :], bound[:, :], P, bass.bass_isa.ReduceOp.max
                                               ).then_inc(s_bound, 1)

            @block.scalar
            def _(act):
                act.wait_ge(s_norm_p, 1)
                nc.scalar.activation(norm[:, :], norm_p[:, :], ACT.Sqrt).then_inc(s_norm, 1)
                act.wait_ge(s_t, 1)
                nc.scalar.copy(g_hi[:, :, :], t[:, :, :]).then_inc(s_hi, 1)

            @block.sync
            def _(sp):
                rounds = attr_rounds(sp)
                with sp.Fori(0, rounds) as r:
                    gate(sp, s_off, r + 1)
                    with sp.Fori(0, NG // AU) as i:
                        for k in range(AU):
                            at = sp.value_load(at_i[0:1, bass.ds(AU * i + k, 1)], min_val=0, max_val=E - ASLOTS)
                            sp.wait_ge(s_summed, (r * (NG // AU) + i) * AU + (k + 1))
                            sp.dma_start(rows[:, k, :, :].rearrange("p c f -> p (c f)"),
                                         attr[bass.ds(at, ASLOTS), :].rearrange("(p c) f -> p (c f)", p=P)
                                         ).then_inc(s_loaded[k], 16)
                            sp.dma_start(adst[:, k, :],
                                         dst_d[bass.ds(at, ASLOTS)].rearrange("(p c) -> p c", p=P)
                                         ).then_inc(s_loaded[k], 16)
                sp.wait_ge(s_done, rounds)
                sp.dma_start(agg_d, agg[:, :]).then_inc(s_agg_d, 16)
                sp.wait_ge(s_agg_d, 16)

            @block.tensor
            def _(pe):
                rounds = attr_rounds(pe)
                pe.sem_inc(s_summed, AU)
                pe.wait_ge(s_square, 2)
                nc.tensor.matmul(norm_p[:, :], square[:, :], ones_p[:, :], start=True, stop=True).then_inc(s_norm_p, 1)
                with pe.Fori(0, rounds) as r:
                    with pe.Fori(0, NG // AU) as i:
                        for k in range(AU):
                            pe.wait_ge(s_loaded[k], (r * (NG // AU) + i + 1) * 32)
                            pe.wait_ge(s_hot, (r * (NG // AU) + i) * AU + (k + 1))
                            pe.wait_ge(s_added, (r * (NG // AU) + i) * AU + (k + 1))
                            for c in range(AC):
                                ins = nc.tensor.matmul(agg_p[k][:, :], rows[:, k, c, :], hot[:, k, c, :],
                                                       start=(c == 0), stop=(c == AC - 1))
                            ins.then_inc(s_summed, 1)

            @block.vector
            def _(dve):
                ch = Chain(dve, s_dve)
                dve.sem_inc(s_added, AU)
                nc.vector.tensor_tensor(square[:, :], W1_sb[:, :], W1_sb[:, :], ALU.mult).then_inc(s_square, 1)
                nc.vector.memset(ones_p[:, :], 1.0).then_inc(s_square, 1)
                dve.wait_ge(s_const, 4)
                ch.link(nc.vector.tensor_copy(want[:, :], gstart[:, 0:NG]))

                def place_loads(n):
                    nc.vector.tensor_scalar(at_f[:, :], want[0:1, :], float(E - ASLOTS), None, ALU.min
                                            ).then_inc(s_round, 1)
                    dve.wait_ge(s_round, n)
                    nc.vector.tensor_copy(at_i[:, :], at_f[:, :]).then_inc(s_off, 1)

                place_loads(1)
                rounds = attr_rounds(dve)

                def add_group(n, g, k):
                    dve.wait_ge(s_summed, n + (AU + 1))
                    nc.vector.tensor_tensor(agg[:, bass.ds(g * GN, GN)], agg[:, bass.ds(g * GN, GN)],
                                            agg_p[k][:, :], ALU.add).then_inc(s_added, 1)

                def hot_group(r, i, k):
                    n = (r * (NG // AU) + i) * AU + k
                    g = AU * i + k
                    dve.wait_ge(s_loaded[k], (r * (NG // AU) + i + 1) * 32)
                    dve.wait_ge(s_summed, n + 1)
                    nc.vector.tensor_scalar(arel[:, k, 0, :], pos[:, :], over[:, bass.ds(g, 1)], BIG,
                                            ALU.is_lt, ALU.mult).then_inc(s_dve, 1)
                    dve.wait_ge(s_dve, 2 * n + 2)
                    nc.vector.scalar_tensor_tensor(out=arel[:, k, 1, :], in0=adst[:, k, :],
                                                   scalar=gbase[:, bass.ds(g, 1)], in1=arel[:, k, 0, :],
                                                   op0=ALU.add, op1=ALU.add).then_inc(s_dve, 1)
                    dve.wait_ge(s_dve, 2 * n + 3)
                    nc.vector.tensor_tensor(hot[:, k, :, :], iota_n[:, :].unsqueeze(1).to_broadcast([P, AC, GN]),
                                            arel[:, k, 1, :].unsqueeze(2).to_broadcast([P, AC, GN]),
                                            ALU.is_equal).then_inc(s_hot, 1)

                LAG = 3
                with dve.Fori(0, rounds) as r:
                    nc.vector.tensor_scalar(over[:, :], want[:, :], -float(E - ASLOTS), 0.0, ALU.add, ALU.max
                                            ).then_inc(s_round, 1)
                    gate(dve, s_round, r * 2 + 2)
                    n0 = r * NG
                    for k in range(AU):
                        hot_group(r, 0, k)
                        if k >= LAG:
                            add_group(n0 + (k - LAG), k - LAG, k - LAG)
                    with dve.Fori(1, NG // AU) as i:
                        for k in range(AU):
                            hot_group(r, i, k)
                            add_group(n0 + i * AU + (k - LAG), i * AU + (k - LAG), (k - LAG) % AU)
                    for k in range(AU - LAG, AU):
                        add_group(n0 + (NG - AU + k), NG - AU + k, k)
                    gate(dve, s_added, (r + 1) * NG + AU)
                    nc.vector.tensor_scalar(want[:, :], want[:, :], float(ASLOTS), None, ALU.add
                                            ).then_inc(s_done, 1)
                    gate(dve, s_done, r + 1)
                    place_loads(r * 2 + 3)
                ch_b = Chain(dve, s_bound)
                dve.wait_ge(s_norm, 1)
                ch_b.link(nc.vector.tensor_scalar(bound[:, :], b1_sb[:, :], -1.0, None, ALU.mult))
                ch_b.link(nc.vector.tensor_tensor(bound[:, :], bound[:, :], b1_sb[:, :], ALU.max))
                ch_b.link(nc.vector.scalar_tensor_tensor(out=bound[:, :], in0=norm[:, :], scalar=float(F) ** 0.5,
                                                         in1=bound[:, :], op0=ALU.mult, op1=ALU.add))
                dve.wait_ge(s_bound, 4)
                ch_b.n = 4
                ch_b.link(nc.vector.tensor_scalar(inv2[:, :], bound[:, :], 1.0 / TOP, 1e-30, ALU.mult, ALU.max))
                nc.vector.reciprocal(scale2[:, :], inv2[:, :])

        operand_ctx.close()

        def load_rounds(eng):
            return eng.value_load(rounds_i[0:1, 0:1], min_val=1, max_val=ROUNDS)

        def aggregate(layer, total):
            with ExitStack() as ph:
                start = sb(f"start{layer}", [TP, FETCHES], F32, ph)
                start_i = sb(f"start_i{layer}", [TP, 2, 2], I32, ph)
                ql = sb(f"ql{layer}", [TP, 2, 2, P, 2], F32, ph)
                code = sb(f"code{layer}", [P, 2, 2, BP, 2], F16, ph)
                mv = sb(f"mv{layer}", [P, 2, GU, UP, MV], F16, ph)
                st = sb(f"st{layer}", [P, 2, GU, UP, P], F16, ph)
                adj = adj_all[:, 0:2 * HI * BN].rearrange("p (b h n) -> p b h n", b=2, h=HI)
                win_p = ps(f"win_p{layer}", [P, 4, 512], ph)
                dense_p = ps(f"dense_p{layer}", [P, 2, 512], ph)
                code_p = ps(f"code_p{layer}", [P, 2, 2, TP], ph)
                fetched = [sem(f"fetched{layer}_{h}", ph) for h in range(2)]
                s_start = sem(f"s_start{layer}", ph)
                indices = sem(f"indices{layer}", ph)
                relative = sem(f"relative{layer}", ph)
                turned = sem(f"turned{layer}", ph)
                codes_ready = sem(f"codes_ready{layer}", ph)
                hot_ready = sem(f"hot_ready{layer}", ph)
                built = sem(f"built{layer}", ph)
                evicted = sem(f"evicted{layer}", ph)
                saved = sem(f"saved{layer}", ph)
                dense_done = sem(f"dense_done{layer}", ph)
                taken = sem(f"taken{layer}", ph)
                zeroed = sem(f"zeroed{layer}", ph)
                block = ph.enter_context(nc.Block())

                def either(eng, build):
                    rounds = load_rounds(eng)
                    if layer == 1:
                        build(eng, rounds)
                    else:
                        with eng.If(rounds > 1):
                            build(eng, rounds)
                        with eng.Else():
                            eng.sem_inc(s_gate, 1)

                @block.gpsimd
                def _(pool):
                    def fetch(r, i, h):
                        gate(pool, turned, r * NB + i * 2 + (h + 1))
                        nc.gpsimd.tensor_copy(start_i[:, h, :], start[:, bass.ds(i * 4 + 2 * h, 2)]
                                              ).then_inc(indices, 1)
                        gate(pool, indices, r * NB + i * 2 + (h + 1))
                        for k in range(2):
                            nc.gpsimd.indirect_dma_start(
                                out=ql[:, h, k, :, :].rearrange("p s t -> p (s t)"), out_offset=None, in_=ql_d,
                                in_offset=bass.IndirectOffsetOnAxis(
                                    ap=start_i[:, h, k:k + 1], axis=0)).then_inc(fetched[h], 16)

                    def subtract(r, i, h):
                        gate(pool, fetched[h], r * (NB // 2 * 32) + i * 32 + 32)
                        nc.gpsimd.tensor_tensor(
                            ql[:, h, :, :, 0], ql[:, h, :, :, 0],
                            pcode[:, bass.ds(i * 4 + 2 * h, 2)].unsqueeze(2).to_broadcast([TP, 2, P]), ALU.subtract
                        ).then_inc(relative, 1)
                        gate(pool, relative, (r * NB + i * 2 + h) * 2 + 1)
                        nc.gpsimd.tensor_scalar(ql[:, h, :, :, 0], ql[:, h, :, :, 0], float(CLIP), None, ALU.min
                                                ).then_inc(relative, 1)

                    def build(pool, rounds):
                        nc.gpsimd.tensor_copy(start[:, :], pstart[:, :]).then_inc(s_start, 1)
                        with pool.Fori(0, rounds) as r:
                            gate(pool, s_start, r + 1)
                            fetch(r, 0, 0)
                            with pool.Fori(0, NB // 2 - 1) as i:
                                fetch(r, i, 1)
                                subtract(r, i, 0)
                                fetch(r, i + 1, 0)
                                subtract(r, i, 1)
                            fetch(r, NB // 2 - 1, 1)
                            for h in range(2):
                                subtract(r, NB // 2 - 1, h)
                            nc.gpsimd.tensor_scalar(start[:, :], start[:, :], float(P), float(E), ALU.add, ALU.min
                                                    ).then_inc(s_start, 1)

                    either(pool, build)

                @block.vector
                def _(dve):
                    def group(r, b, j):
                        n = r * NW + b * (BG * GW) + j * GW
                        gate(dve, codes_ready, r * NB + b + 2)
                        for u in range(GU):
                            pairs = bass.ds(j * (GU * UP) + u * UP, UP)
                            dve.wait_ge(built, n + (u + 1) * UW)
                            for hot, iota, t, width in ((st, iota_lo, 1, P), (mv, iota_mv, 0, MV)):
                                ins = nc.vector.tensor_tensor(
                                    hot[:, bass.ds((b * BG + j) % 2, 1), u, :, :]
                                    .rearrange("p a w (n t) -> p (a w) n t", t=2),
                                    iota[:, :].rearrange("p (n t) -> p n t", t=2).unsqueeze(1)
                                    .to_broadcast([P, UP, width // 2, 2]),
                                    code[:, bass.ds(b % 2, 1), t, pairs, :].rearrange("p a w t -> p (a w) t")
                                    .unsqueeze(2).to_broadcast([P, UP, width // 2, 2]), ALU.is_equal)
                            ins.then_inc(hot_ready, 1)

                    def add_block(r, b):
                        dve.wait_ge(dense_done, r * NB + b + 2)
                        nc.vector.tensor_tensor(
                            total[:, bass.ds(b * BN, BN)], total[:, bass.ds(b * BN, BN)],
                            dense_p[:, bass.ds(b % 2, 1), 0:BN].rearrange("p b n -> p (b n)"), ALU.add
                        ).then_inc(taken, 1)

                    def build(dve, rounds):
                        nc.vector.memset(total[:, :], 0.0).then_inc(zeroed, 1)
                        gate(dve, zeroed, 1)
                        dve.sem_inc(taken, 2)
                        with dve.Fori(0, rounds) as r:
                            with dve.Fori(0, 2) as b:
                                with dve.Fori(0, BG) as j:
                                    group(r, b, j)
                            with dve.Fori(2, NB) as b:
                                with dve.Fori(0, 2) as j:
                                    group(r, b, j)
                                add_block(r, b - 2)
                                with dve.Fori(2, BG) as j:
                                    group(r, b, j)
                            add_block(r, NB - 2)
                            add_block(r, NB - 1)

                    either(dve, build)

                @block.scalar
                def _(act):
                    def take_codes(r, b):
                        gate(act, turned, r * NB + b + 3)
                        gate(act, hot_ready, (r * NB + b) * (BG * GU) + 1)
                        nc.scalar.copy(
                            code[:, bass.ds(b % 2, 1), :, :, :].rearrange("p a t w d -> p (a t w) d"),
                            code_p[:, :, :, :].rearrange("p t k w -> p (t k w)").unsqueeze(2)
                            .to_broadcast([P, 2 * BP, 2])).then_inc(codes_ready, 1)

                    def evict_block(r, b):
                        with act.Fori(0, BG) as j:
                            for k in range(GW):
                                gate(act, built, r * NW + b * (BG * GW) + j * GW + (2 * GW + k + 1))
                                nc.scalar.copy(
                                    adj[:, bass.ds(b % 2, 1), :, bass.ds(j * GN + k * WN, WN)]
                                    .rearrange("p b h d -> p d (b h)"),
                                    win_p[:, k % 4, 0:WP * MV].rearrange("p (d h) -> p d h", d=WN)
                                ).then_inc(evicted, 1)
                        if layer == 1:
                            gate(act, saved, (r * NB + b) * 16 + 16)
                            gate(act, evicted, r * NW + b * (BG * GW) + (BG * GW + 4))
                            act.dma_start(adj_d[:, :, bass.ds(b * BN, BN)],
                                          adj[:, bass.ds(b % 2, 1), :, :].rearrange("p b h n -> p (b h) n")
                                          ).then_inc(saved, 16)

                    def build(act, rounds):
                        act.sem_inc(evicted, 4)
                        act.sem_inc(saved, 16)
                        act.sem_inc(hot_ready, 2 * BG * GU)
                        act.sem_inc(codes_ready, 1)
                        with act.Fori(0, rounds) as r:
                            take_codes(r, 0)
                            with act.Fori(0, NB - 1) as b:
                                take_codes(r, b + 1)
                                evict_block(r, b)
                            evict_block(r, NB - 1)
                        if layer == 1:
                            gate(act, saved, rounds * (NB * 16) + 16)

                    either(act, build)

                @block.tensor
                def _(pe):
                    def turn_codes(r, b, h):
                        gate(pe, relative, r * (2 * NB) + b * 2 + 2)
                        gate(pe, codes_ready, r * NB + b + 1)
                        for k in range(2):
                            for t in range(2):
                                ins = nc.tensor.transpose(code_p[:, t, k, :],
                                                            ql[:, h, k, :, t], ident[0:TP, 0:TP])
                        ins.then_inc(turned, 1)

                    def build_window(r, i, odd, k):
                        n = r * NW + i * GW + (k + 1)
                        if k % UW == 0:
                            pe.wait_ge(hot_ready, (r * NG + i) * GU + (k // UW + 1 + 2 * BG * GU))
                        pe.wait_ge(evicted, n)
                        for c in range(WP):
                            pair = k % UW * WP + c
                            ins = nc.tensor.matmul(win_p[:, k % 4, c * MV:(c + 1) * MV],
                                                   st[:, odd, k // UW, pair, :], mv[:, odd, k // UW, pair, :],
                                                   start=True, stop=True)
                        ins.then_inc(built, 1)

                    def open_block(r, b):
                        gate(pe, evicted, r * NW + b * (BG * GW) + (BG * GW + 4))
                        gate(pe, taken, r * NB + b + 1)

                    def multiply(half, j, k):
                        c = j * HG + k
                        for g in (g_hi, g_lo):
                            ins = nc.tensor.matmul(dense_p[:, half, 0:BN], g[:, c, :], adj[:, half, c, :],
                                                   start=(c == 0 and g is g_hi), stop=(c == HI - 1 and g is g_lo))
                        if c == HI - 1:
                            ins.then_inc(dense_done, 1)

                    def build(pe, rounds):
                        pe.sem_inc(built, 2 * GW)
                        pe.sem_inc(turned, 2)
                        pe.sem_inc(dense_done, 1)

                        def build_and_multiply(r, b, half):
                            for j in range(BG):
                                for k in range(GW):
                                    build_window(r, b * BG + j, (1 - half + j) % 2, k)
                                    if j == 0 and k == GW - HG:
                                        open_block(r, b - 1)
                                    if k >= GW - HG:
                                        multiply(half, j, k - (GW - HG))

                        with pe.Fori(0, rounds) as r:
                            turn_codes(r, 0, 0)
                            turn_codes(r, 1, 1)
                            for j in range(BG):
                                for k in range(GW):
                                    build_window(r, j, j % 2, k)
                            with pe.Fori(0, NB // 2 - 1) as i:
                                for h in range(2):
                                    turn_codes(r, i * 2 + (2 + h), h)
                                    build_and_multiply(r, i * 2 + (1 + h), h)
                            build_and_multiply(r, NB - 1, 0)
                            open_block(r, NB - 1)
                            for j in range(BG):
                                for k in range(HG):
                                    multiply(1, j, k)

                    either(pe, build)

        def first_layer_end(total):
            with ExitStack() as ph:
                cur = sb("cur", [P, 4, TB * P], F32, ph)
                disb = sb("disb", [P, 4, TB * P], F32, ph)
                hn = total
                s_adj = sem("s_adj_e", ph)
                sdis = sb("sdis2", [P, HI], F32, ph)
                lin_p = ps("lin_p1", [P, 2, 512], ph)
                tp = ps("tp_e", [P, 4, TB, P], ph)
                s_cur = [sem(f"s_cur{k}", ph) for k in range(4)]
                s_own = sem("s_own", ph)
                s_mixed = sem("s_mixed", ph)
                s_lin = sem("s_lin", ph)
                s_hn = sem("s_hn", ph)
                s_turned = sem("s_turned_e", ph)
                s_hi = sem("s_hi_e", ph)
                s_lo = sem("s_lo_e", ph)
                s_out = sem("s_out_e", ph)
                s_dve = sem("s_dve_e", ph)
                block = ph.enter_context(nc.Block())

                @block.sync
                def _(sp):
                    def store(i):
                        k, n = BATCH[i]
                        cols = slice(k * P, (k + n) * P)
                        sp.wait_ge(s_hn, i + 1)
                        sp.dma_start(h1T_d[:, cols], hn[:, cols]).then_inc(s_out, 16)

                    for i, (k, n) in enumerate(BATCH):
                        cols = slice(k * P, (k + n) * P)
                        if i >= 4:
                            sp.wait_ge(s_mixed, i - 3)
                        sp.dma_start(disb[:, i % 4, 0:n * P],
                                     dis_d[cols].rearrange("(a n) -> a n", a=1).to_broadcast([P, n * P])
                                     ).then_inc(s_cur[i % 4], 16)
                        sp.dma_start(cur[:, i % 4, 0:n * P], hT_d[:, cols]).then_inc(s_cur[i % 4], 16)
                        if 4 <= i < 4 + BG:
                            part = slice((i - 4) * HG, (i - 3) * HG)
                            sp.dma_start(adj_in[:, 0, part, :], adj_d[:, part, 0:CW]).then_inc(s_adj, 16)
                    for i in range(len(BATCH)):
                        store(i)
                    sp.wait_ge(s_adj, 16 * BG)
                    sp.wait_ge(s_out, 16 * len(BATCH))

                @block.gpsimd
                def _(pool):
                    for i, (k, n) in enumerate(BATCH):
                        c, d = cur[:, i % 4, 0:n * P], disb[:, i % 4, 0:n * P]
                        pool.wait_ge(s_cur[i % 4], 32 * (i // 4 + 1))
                        nc.gpsimd.tensor_tensor(c, c, d, ALU.mult).then_inc(s_own, 1)

                @block.vector
                def _(dve):
                    ch = Chain(dve, s_dve)
                    ch.link(nc.vector.tensor_scalar(sdis[:, :], dis[:, :], scale2[:, 0:1], None, ALU.mult))

                    def mix(i):
                        k, n = BATCH[i]
                        cols = slice(k * P, (k + n) * P)
                        c, d = cur[:, i % 4, 0:n * P], disb[:, i % 4, 0:n * P]
                        dve.wait_ge(s_own, i + 1)
                        ch.link(nc.vector.scalar_tensor_tensor(out=total[:, cols], in0=total[:, cols],
                                                               scalar=inv[:, 0:1], in1=c,
                                                               op0=ALU.mult, op1=ALU.add))
                        nc.vector.tensor_tensor(total[:, cols], total[:, cols], d, ALU.mult).then_inc(s_mixed, 1)

                    def low(i):
                        k, n = BATCH[i]
                        dve.wait_ge(s_hi, i + 1)
                        for c in range(n):
                            ins = nc.vector.scalar_tensor_tensor(
                                out=g_lo[:, k + c, :], in0=tp[:, i % 4, c, :], scalar=sdis[:, k + c:k + c + 1],
                                in1=g_hi[:, k + c, :], op0=ALU.mult, op1=ALU.subtract)
                        ins.then_inc(s_lo, 1)

                    LATE = 3
                    for i in range(len(BATCH) + LATE):
                        if i < len(BATCH):
                            mix(i)
                        if i >= LATE:
                            low(i - LATE)

                @block.scalar
                def _(act):
                    def high(i):
                        k, n = BATCH[i]
                        act.wait_ge(s_turned, i + 1)
                        for c in range(n):
                            ins = nc.scalar.activation(g_hi[:, k + c, :], tp[:, i % 4, c, :], ACT.Identity,
                                                       scale=sdis[:, k + c:k + c + 1])
                        ins.then_inc(s_hi, 1)

                    for i, (k, n) in enumerate(BATCH):
                        act.wait_ge(s_lin, i + 1)
                        nc.scalar.activation(hn[:, k * P:(k + n) * P], lin_p[:, i % 2, 0:n * P], ACT.Relu,
                                             bias=b1_sb[:, 0:1]).then_inc(s_hn, 1)
                        if i >= 1:
                            high(i - 1)
                    high(len(BATCH) - 1)

                @block.tensor
                def _(pe):
                    def turn(i):
                        k, n = BATCH[i]
                        pe.wait_ge(s_hn, i + 1)
                        if i >= 4:
                            pe.wait_ge(s_lo, i - 3)
                        for c in range(n):
                            ins = nc.tensor.transpose(tp[:, i % 4, c, :], hn[:, (k + c) * P:(k + c + 1) * P],
                                                      ident[:, :])
                        ins.then_inc(s_turned, 1)

                    for i, (k, n) in enumerate(BATCH):
                        pe.wait_ge(s_mixed, i + 1)
                        if i >= 2:
                            pe.wait_ge(s_hn, i - 1)
                        nc.tensor.matmul(lin_p[:, i % 2, 0:n * P], W1_sb[:, :], total[:, k * P:(k + n) * P],
                                         start=True, stop=True).then_inc(s_lin, 1)
                        if i >= 1:
                            turn(i - 1)
                    turn(len(BATCH) - 1)

        def second_layer_and_mlp():
            M1, M2 = w1.shape[1] // P, w2.shape[1] // P
            assert M1 == M2
            KU = F + EF
            SLOPE = 0.01
            NC = HI // NT
            SMALL = 5
            assert HI == NC * NT + 1 and NC % 2 == 0
            with ExitStack() as ph:
                tot = sb("tot", [P, 2, CW], F32, ph)
                cur = sb("cur2", [P, 2, CW], F32, ph)
                h0 = sb("h0", [P, 2, CW], F32, ph)
                disb = sb("disb2", [P, 2, CW], F32, ph)
                agg = sb("agg2", [EF, 2, CW], F32, ph)
                xt = sb("xt", [P, 2, NT, F], F32, ph)
                mix = sb("mix", [P, CW], F32, ph)
                hn = sb("hn2", [P, CW], F32, ph)
                stats = sb("stats", [P, NT, 6], F32, ph)
                mean_var = sb("mean_var", [P, NT, 2], F32, ph)
                var = sb("var2", [P, NT], F32, ph)
                root = sb("root2", [P, NT], F32, ph)
                rstd = sb("rstd", [P, NT], F32, ph)
                tmp = sb("tmp2", [P, NT], F32, ph)
                shift = sb("shift", [P, NT], F32, ph)
                hl = sb("hl", [P, NT, F], F32, ph)
                hT = sb("hT2", [P, CW], F32, ph)
                z1 = sb("z1", [P, M1, CW], F32, ph)
                a1 = sb("a1", [P, M1, CW], F32, ph)
                z2 = sb("z2", [P, M2, CW], F32, ph)
                a2 = sb("a2", [P, M2, CW], F32, ph)
                W_sb = sb("W2_sb", [P, F], F32, ph)
                b_sb = sb("b2_sb", [P, 1], F32, ph)
                w1a = sb("w1a", [P, M1 * P], F32, ph)
                w1b = sb("w1b", [EF, M1 * P], F32, ph)
                w1u = sb("w1u", [EF, M1 * P], F32, ph)
                w2_sb = sb("w2_sb", [P, M1, M2 * P], F32, ph)
                w3_sb = sb("w3_sb", [P, M2, F], F32, ph)
                u_sb = sb("u_sb", [EF, 1], F32, ph)
                c1_sb = sb("c1_sb", [P, M1], F32, ph)
                c2_sb = sb("c2_sb", [P, M2], F32, ph)
                c3_sb = sb("c3_sb", [1, F], F32, ph)
                dense_p = ps("dense_p_b", [P, 2, 512], ph)
                lin_p = ps("lin_p2", [P, 512], ph)
                tpa = ps("tpa", [P, NT, F], ph)
                tpb = ps("tpb", [P, NT, P], ph)
                zz_p = ps("zz_p", [P, M1, 512], ph)
                y_p = ps("y_p", [P, NT, F], ph)
                s_w = sem("s_w2", ph)
                s_uc = sem("s_uc", ph)
                s_c1 = sem("s_c1", ph)
                s_pad = sem("s_pad2", ph)
                adj_ready = [sem(f"adj_ready{h}", ph) for h in range(2)]
                small_ready = [sem(f"small_ready{h}", ph) for h in range(2)]
                stored = [sem(f"stored{h}", ph) for h in range(2)]
                dense_done = sem("dense_done_b", ph)
                tot_ready = sem("tot_ready", ph)
                mixed = sem("mixed", ph)
                lin_done = sem("lin_done", ph)
                hn_ready = sem("hn_ready", ph)
                comb_ready = sem("comb_ready", ph)
                tpa_done = sem("tpa_done", ph)
                var_ready = sem("var_ready", ph)
                root_ready = sem("root_ready", ph)
                shift_ready = sem("shift_ready", ph)
                hl_ready = sem("hl_ready", ph)
                tpb_done = sem("tpb_done", ph)
                hT_ready = sem("hT_ready", ph)
                z1p_done = sem("z1p_done", ph)
                z1_ready = sem("z1_ready", ph)
                a1_ready = sem("a1_ready", ph)
                z2p_done = sem("z2p_done", ph)
                z2_ready = sem("z2_ready", ph)
                a2_ready = sem("a2_ready", ph)
                y_done = sem("y_done", ph)
                y_added = sem("y_added", ph)
                s_chain = sem("s_chain", ph)
                CHAIN = 16 + 3 * NT
                block = ph.enter_context(nc.Block())

                def two_before(i):
                    return not (isinstance(i, int) and i == 0)

                def by_rounds(eng, program):
                    with eng.If(load_rounds(eng) > 1):
                        program(eng, False)
                    with eng.Else():
                        program(eng, True)

                @block.sync
                def _(sp):
                    sp.dma_start(W_sb[:, :], W2).then_inc(s_w, 16)
                    sp.dma_start(w1a[:, :], w1[0:F, :]).then_inc(s_w, 16)
                    sp.dma_start(w1b[:, :], w1[F:KU, :]).then_inc(s_w, 16)
                    sp.dma_start(w1u[:, :], w1[KU:KU + EF, :]).then_inc(s_w, 16)
                    sp.dma_start(w2_sb[:, :, :], w2.rearrange("(m p) n -> p m n", p=P)).then_inc(s_w, 16)
                    sp.dma_start(w3_sb[:, :, :], w3.rearrange("(m p) n -> p m n", p=P)).then_inc(s_w, 16)
                    sp.dma_start(c3_sb[:, :], c3.rearrange("(a n) -> a n", a=1)).then_inc(s_w, 16)
                    with nc.allow_non_contiguous_dma(reason="vectors, one element per partition"):
                        sp.dma_start(b_sb[:, :], b2.rearrange("(p a) -> p a", a=1)).then_inc(s_w, 16)
                        sp.dma_start(u_sb[:, :], u[0:1, :].rearrange("a n -> n a")).then_inc(s_w, 16)
                        sp.dma_start(c1_sb[:, :], c1.rearrange("(m p) -> p m", p=P)).then_inc(s_w, 16)
                        sp.dma_start(c2_sb[:, :], c2.rearrange("(m p) -> p m", p=P)).then_inc(s_w, 16)

                    def program(sp, one_round):
                        def load(i, h, n):
                            c = i * 2 + h
                            w = n * P
                            cols = bass.ds(c * CW, w)
                            if one_round:
                                gate(sp, dense_done, c + 1)
                                if h == 0 and not two_before(i):
                                    sp.sem_inc(adj_ready[0], 16)
                                else:
                                    sp.dma_start(adj_in[:, h, :, 0:w], adj_d[:, :, cols]).then_inc(adj_ready[h], 16)
                            if two_before(i):
                                gate(sp, y_added, c + 1)
                                gate(sp, stored[h], i * 16)
                            sp.dma_start(cur[:, h, 0:w], h1T_d[:, cols]).then_inc(small_ready[h], 16)
                            sp.dma_start(h0[:, h, 0:w], hT_d[:, cols]).then_inc(small_ready[h], 16)
                            sp.dma_start(disb[:, h, 0:w],
                                         dis_d[cols].rearrange("(a n) -> a n", a=1).to_broadcast([P, w])
                                         ).then_inc(small_ready[h], 16)
                            sp.dma_start(agg[:, h, 0:w], agg_d[:, cols]).then_inc(small_ready[h], 16)
                            if n == NT:
                                sp.dma_start(xt[:, h, :, :],
                                             x[bass.ds(c * CW, CW), :].rearrange("(c p) f -> p c f", p=P)
                                             ).then_inc(small_ready[h], 16)
                            else:
                                sp.wait_ge(s_pad, 1)
                                sp.dma_start(xt[0:TAIL, h, 0, :], x[(HI - 1) * P:N, :]).then_inc(small_ready[h], 16)
                            if not one_round:
                                sp.dma_start(tot[:, h, 0:w], total_d[:, cols]).then_inc(small_ready[h], 16)

                        for h in range(2):
                            load(0, h, NT)
                        with sp.Fori(1, NC // 2) as i:
                            for h in range(2):
                                load(i, h, NT)
                        load(NC // 2, 0, 1)

                    by_rounds(sp, program)

                @block.gpsimd
                def _(pool):
                    with pool.Fori(0, NC // 2) as i:
                        for h in range(2):
                            c = i * 2 + h
                            gate(pool, y_added, c + 3)
                            pool.dma_start(out[bass.ds(c * CW, CW), :].rearrange("(c p) f -> p c f", p=P),
                                           xt[:, h, :, :]).then_inc(stored[h], 16)
                    pool.wait_ge(y_added, NC + 3)
                    pool.dma_start(out[(HI - 1) * P:N, :], xt[0:TAIL, 0, 0, :]).then_inc(stored[0], 16)
                    for h in range(2):
                        pool.wait_ge(stored[h], 16 * (NC // 2 + 1 - h))

                @block.vector
                def _(dve):
                    dve.sem_inc(y_added, 2)
                    dve.sem_inc(mixed, 2)
                    dve.wait_ge(s_w, 16 * 11)
                    dve.wait_ge(s_uc, 1)
                    nc.vector.tensor_tensor(c1_sb[:, :], c1_sb[:, :], lin_p[:, 0:M1], ALU.add).then_inc(s_c1, 1)

                    def program(dve, one_round):
                        def finish(i, h, n):
                            c = i * 2 + h
                            w = n * P
                            step = [0]

                            def link(ins):
                                step[0] += 1
                                ins.then_inc(s_chain, 1)
                                dve.wait_ge(s_chain, c * CHAIN + step[0])

                            dve.wait_ge(small_ready[h], (i + 1) * (16 * (SMALL if one_round else SMALL + 1)))
                            link(nc.vector.tensor_tensor(cur[:, h, 0:w], cur[:, h, 0:w], disb[:, h, 0:w], ALU.mult))
                            if one_round:
                                dve.wait_ge(tot_ready, c + 1)
                            link(nc.vector.scalar_tensor_tensor(out=mix[:, 0:w], in0=tot[:, h, 0:w],
                                                                scalar=inv2[:, 0:1], in1=cur[:, h, 0:w],
                                                                op0=ALU.mult, op1=ALU.add))
                            nc.vector.tensor_tensor(mix[:, 0:w], mix[:, 0:w], disb[:, h, 0:w], ALU.mult
                                                    ).then_inc(mixed, 1)
                            dve.wait_ge(hn_ready, c + 1)
                            nc.vector.tensor_tensor(hn[:, 0:w], hn[:, 0:w], h0[:, h, 0:w], ALU.add
                                                    ).then_inc(comb_ready, 1)
                            dve.wait_ge(tpa_done, c + 1)
                            link(nc.vector.scalar_tensor_tensor(out=xt[:, h, 0:n, :], in0=tpa[:, 0:n, :], scalar=0.5,
                                                                in1=xt[:, h, 0:n, :], op0=ALU.mult, op1=ALU.add))
                            for k in range(n):
                                step[0] += 1
                                nc.vector.bn_stats(stats[:, k, :], xt[:, h, k, :]).then_inc(s_chain, 1)
                            gate(dve, s_chain, c * CHAIN + step[0])
                            for k in range(n):
                                step[0] += 1
                                nc.vector.bn_aggr(mean_var[:, k, :], stats[:, k, :]).then_inc(s_chain, 1)
                            dve.wait_ge(s_chain, c * CHAIN + step[0])
                            nc.vector.tensor_scalar(var[:, 0:n], mean_var[:, 0:n, 1], EPS, None, ALU.add
                                                    ).then_inc(var_ready, 1)
                            dve.wait_ge(root_ready, c + 1)
                            link(nc.vector.reciprocal(rstd[:, 0:n], root[:, 0:n]))
                            link(nc.vector.tensor_tensor(tmp[:, 0:n], rstd[:, 0:n], rstd[:, 0:n], ALU.mult))
                            link(nc.vector.tensor_tensor(tmp[:, 0:n], tmp[:, 0:n], var[:, 0:n], ALU.mult))
                            link(nc.vector.tensor_scalar(tmp[:, 0:n], tmp[:, 0:n], -0.5, 1.5, ALU.mult, ALU.add))
                            link(nc.vector.tensor_tensor(rstd[:, 0:n], rstd[:, 0:n], tmp[:, 0:n], ALU.mult))
                            nc.vector.scalar_tensor_tensor(out=shift[:, 0:n], in0=mean_var[:, 0:n, 0], scalar=-1.0,
                                                           in1=rstd[:, 0:n], op0=ALU.mult, op1=ALU.mult
                                                           ).then_inc(shift_ready, 1)
                            dve.wait_ge(tpb_done, c + 1)
                            nc.vector.tensor_copy(hT[:, 0:w], tpb[:, 0:n, :].rearrange("p n f -> p (n f)")
                                                  ).then_inc(hT_ready, 1)
                            for z, a, z_ready, a_ready in ((z1, a1, z1_ready, a1_ready), (z2, a2, z2_ready, a2_ready)):
                                dve.wait_ge(z_ready, c + 1)
                                nc.vector.scalar_tensor_tensor(out=a[:, :, 0:w], in0=z[:, :, 0:w], scalar=SLOPE,
                                                               in1=z[:, :, 0:w], op0=ALU.mult, op1=ALU.max
                                                               ).then_inc(a_ready, 1)
                            assert step[0] <= CHAIN
                            dve.sem_inc(s_chain, CHAIN - step[0])
                            dve.wait_ge(y_done, c + 1)
                            nc.vector.tensor_tensor(xt[:, h, 0:n, :], xt[:, h, 0:n, :], y_p[:, 0:n, :], ALU.add
                                                    ).then_inc(y_added, 1)

                        with dve.Fori(0, NC // 2) as i:
                            for h in range(2):
                                finish(i, h, NT)
                        dve.wait_ge(stored[0], 16 * (NC // 2))
                        nc.vector.memset(xt[:, 0, 0, :], 0.0).then_inc(s_pad, 1)
                        finish(NC // 2, 0, 1)

                    by_rounds(dve, program)

                @block.scalar
                def _(act):
                    act.wait_ge(s_w, 16 * 11)
                    act.wait_ge(s_c1, 1)

                    def program(act, one_round):
                        def take(i, h, n):
                            c = i * 2 + h
                            gate(act, dense_done, c + 3)
                            act.wait_ge(mixed, c + 1)
                            nc.scalar.copy(tot[:, h, 0:n * P], dense_p[:, h, 0:n * P]).then_inc(tot_ready, 1)

                        def finish(i, h, n):
                            c = i * 2 + h
                            w = n * P
                            gate(act, lin_done, c + 1)
                            nc.scalar.activation(hn[:, 0:w], lin_p[:, 0:w], ACT.Relu, bias=b_sb[:, 0:1]
                                                 ).then_inc(hn_ready, 1)
                            gate(act, var_ready, c + 1)
                            nc.scalar.activation(root[:, 0:n], var[:, 0:n], ACT.Sqrt).then_inc(root_ready, 1)
                            gate(act, shift_ready, c + 1)
                            for k in range(n):
                                ins = nc.scalar.activation(hl[:, k, :], xt[:, h, k, :], ACT.Relu,
                                                           bias=shift[:, k:k + 1], scale=rstd[:, k:k + 1])
                            ins.then_inc(hl_ready, 1)
                            for z, bias, zp_done, z_ready in ((z1, c1_sb, z1p_done, z1_ready),
                                                              (z2, c2_sb, z2p_done, z2_ready)):
                                gate(act, zp_done, c + 1)
                                for q in range(M1):
                                    ins = nc.scalar.activation(z[:, q, 0:w], zz_p[:, q, 0:w], ACT.Identity,
                                                               bias=bias[:, q:q + 1])
                                ins.then_inc(z_ready, 1)

                        with act.Fori(0, NC // 2) as i:
                            for h in range(2):
                                if one_round:
                                    take(i, h, NT)
                                finish(i, h, NT)
                        if one_round:
                            take(NC // 2, 0, 1)
                        finish(NC // 2, 0, 1)

                    by_rounds(act, program)

                @block.tensor
                def _(pe):
                    pe.sem_inc(dense_done, 2)

                    def u_product():
                        pe.wait_ge(s_w, 16 * 11)
                        for q in range(M1):
                            ins = nc.tensor.matmul(lin_p[:, q:q + 1], w1u[:, q * P:(q + 1) * P], u_sb[:, :],
                                                   start=True, stop=True)
                        ins.then_inc(s_uc, 1)
                        pe.wait_ge(s_c1, 1)

                    def stages(i, h, n):
                        c = i * 2 + h
                        w = n * P

                        def linear():
                            pe.wait_ge(mixed, c + 3)
                            nc.tensor.matmul(lin_p[:, 0:w], W_sb[:, :], mix[:, 0:w], start=True, stop=True
                                             ).then_inc(lin_done, 1)

                        def turn_to_nodes():
                            pe.wait_ge(comb_ready, c + 1)
                            for k in range(n):
                                ins = nc.tensor.transpose(tpa[:, k, :], hn[:, k * P:(k + 1) * P], ident[:, :])
                            ins.then_inc(tpa_done, 1)

                        def turn_back():
                            pe.wait_ge(hl_ready, c + 1)
                            for k in range(n):
                                ins = nc.tensor.transpose(tpb[:, k, :], hl[:, k, :], ident[:, :])
                            ins.then_inc(tpb_done, 1)

                        def mlp1():
                            pe.wait_ge(hT_ready, c + 1)
                            for q in range(M1):
                                nc.tensor.matmul(zz_p[:, q, 0:w], w1a[:, q * P:(q + 1) * P], hT[:, 0:w],
                                                 start=True, stop=False)
                                ins = nc.tensor.matmul(zz_p[:, q, 0:w], w1b[:, q * P:(q + 1) * P], agg[:, h, 0:w],
                                                       start=False, stop=True)
                            ins.then_inc(z1p_done, 1)

                        def mlp2():
                            pe.wait_ge(a1_ready, c + 1)
                            for q in range(M2):
                                for k in range(M1):
                                    ins = nc.tensor.matmul(zz_p[:, q, 0:w], w2_sb[:, k, q * P:(q + 1) * P],
                                                           a1[:, k, 0:w], start=(k == 0), stop=(k == M1 - 1))
                            ins.then_inc(z2p_done, 1)

                        def mlp3():
                            pe.wait_ge(a2_ready, c + 1)
                            for v in range(n):
                                nc.tensor.matmul(y_p[:, v, :], ones[:, :], c3_sb[:, :], start=True, stop=False)
                                for k in range(M2):
                                    ins = nc.tensor.matmul(y_p[:, v, :], a2[:, k, v * P:(v + 1) * P], w3_sb[:, k, :],
                                                           start=False, stop=(k == M2 - 1))
                            ins.then_inc(y_done, 1)

                        def pause():
                            pass

                        return [linear, turn_to_nodes, pause, turn_back, mlp1, mlp2, mlp3]

                    def multiply(i, h, n, between):
                        c = i * 2 + h
                        pe.wait_ge(adj_ready[h], (i + 1) * 16)
                        if two_before(i):
                            gate(pe, tot_ready, c - 1)
                        for k in range(HI):
                            for g in (g_hi, g_lo):
                                ins = nc.tensor.matmul(dense_p[:, h, 0:n * P], g[:, k, :], adj_in[:, h, k, 0:n * P],
                                                       start=(k == 0 and g is g_hi),
                                                       stop=(k == HI - 1 and g is g_lo))
                            if k % HG == HG - 1 and k // HG < len(between):
                                between[k // HG]()
                        ins.then_inc(dense_done, 1)

                    def program(pe, one_round):
                        if one_round:
                            multiply(0, 0, NT, [u_product])
                            multiply(0, 1, NT, stages(0, 0, NT))
                            with pe.Fori(1, NC // 2) as i:
                                multiply(i, 0, NT, stages(i - 1, 1, NT))
                                multiply(i, 1, NT, stages(i, 0, NT))
                            multiply(NC // 2, 0, 1, stages(NC // 2 - 1, 1, NT))
                        else:
                            u_product()
                            with pe.Fori(0, NC // 2) as i:
                                for h in range(2):
                                    for stage in stages(i, h, NT):
                                        stage()
                        for stage in stages(NC // 2, 0, 1):
                            stage()

                    by_rounds(pe, program)

        def store_total(total):
            with ExitStack() as ph:
                s_total = sem("s_total", ph)
                block = ph.enter_context(nc.Block())

                @block.sync
                def _(sp):
                    with sp.If(load_rounds(sp) > 1):
                        sp.dma_start(total_d, total[:, :]).then_inc(s_total, 16)
                        sp.wait_ge(s_total, 16)
                    with sp.Else():
                        sp.sem_inc(s_gate, 1)

        total_d = scratch("total_d", (P, NP), F32)
        adj_all = sb("adj_all", [P, 2 * HI * CW], F16)
        adj_in = adj_all[:, :].rearrange("p (b h n) -> p b h n", b=2, h=HI)
        with ExitStack() as ly:
            total = sb("total", [P, NP], F32, ly)
            aggregate(1, total)
            first_layer_end(total)
            aggregate(2, total)
            store_total(total)
        second_layer_and_mlp()


_INS = ['x', 'src', 'dst', 'edge_attr_64', 'L0_gnn_W1', 'L0_gnn_b1', 'L0_gnn_W2', 'L0_gnn_b2', 'L1_gnn_u',
        'L1_gnn_w1', 'L1_gnn_b1', 'L1_gnn_w2', 'L1_gnn_b2', 'L1_gnn_w3', 'L1_gnn_b3']


def kernel(**inputs):
    import numpy as _np
    import concourse.bacc as _bacc
    from concourse import mybir as _mybir
    from concourse.bass_utils import run_bass_kernel_spmd as _run

    nc = _bacc.Bacc("TRN2", target_bir_lowering=False, num_devices=1)
    arrays, args = {}, []
    for name in _INS:
        a = _np.ascontiguousarray(inputs[name])
        arrays[f"in_{name}_dram"] = a
        args.append(nc.dram_tensor(f"in_{name}_dram", a.shape, _mybir.dt.from_np(a.dtype), kind="ExternalInput").ap())
    out = nc.dram_tensor("out_0_dram", (6250, 128), _mybir.dt.float32, kind="ExternalOutput").ap()
    build(nc, *args, out)
    r = _run(nc, [arrays], core_ids=[0])
    return r.results[0]["out_0_dram"]
```
